# Optimizing a Trainium2 kernel written in Bass

```python
import numpy as np
import jax
import jax.numpy as jnp

def _softmax(x, axis=-1):
    return jax.nn.softmax(x, axis=axis)

def _gelu(x):
    return jax.nn.gelu(x, approximate=True)

def _silu(x):
    return jax.nn.silu(x)

def _sigmoid(x):
    return jax.nn.sigmoid(x)

def _layernorm(x, axis=-1, eps=1e-05):
    m = jnp.mean(x, axis=axis, keepdims=True)
    v = jnp.var(x, axis=axis, keepdims=True)
    return (x - m) / jnp.sqrt(v + eps)

def _scatter_add(tgt, idx, src, axis=0):
    return tgt.at[idx].add(src)

def _segment_sum(src, seg, n):
    return jax.ops.segment_sum(src, seg, n)
kernel_name = 'mk_decoder_preln_d1_seqx_r4_d077a1'

def setup_inputs(seed: int=0):
    np.random.seed(seed)
    _w = jnp.asarray

    def _rec_inputs():
        import jax
        import jax.numpy as jnp
        _rk = jax.random.key(seed)
        x = -0.000125 + 0.9999 * jax.random.normal(jax.random.fold_in(_rk, 1), (8, 512, 512), jnp.float32)
        _lenS = 512 - jax.random.randint(jax.random.fold_in(_rk, 7), (8,), 0, max(1, 512 // 4) + 1, jnp.int32)
        _lenS2 = 64 - jax.random.randint(jax.random.fold_in(_rk, 8), (8,), 0, max(1, 64 // 4) + 1, jnp.int32)
        _ctx_2048P = jax.random.normal(jax.random.fold_in(_rk, 11), (8, 16, 512), jnp.float32)
        _ctx_2048c = jax.random.dirichlet(jax.random.fold_in(_rk, 511), 0.3 * jnp.ones((16,), jnp.float32), (8, 64))
        _ctx_2048t = jnp.einsum('bsk,bkd->bsd', _ctx_2048c, _ctx_2048P)
        _ctx_2048t = _ctx_2048t * jax.lax.rsqrt(jnp.mean(jnp.square(_ctx_2048t)) + 1e-12) * 0.953939
        ctx_2048 = -0.000514642 + 1.00011 * (_ctx_2048t + 0.3 * jax.random.normal(jax.random.fold_in(_rk, 611), (8, 64, 512), jnp.float32))
        _validS = jnp.arange(512)[None, :] < _lenS[:, None]
        _validS2 = jnp.arange(64)[None, :] < _lenS2[:, None]
        _causal = jnp.tril(jnp.ones((512, 512), dtype=bool))
        mask_BxS2_bk0 = jnp.logical_not(jnp.broadcast_to(_validS2[:, :], (8, 64)))
        return (x, ctx_2048, mask_BxS2_bk0)
    x, ctx_2048, mask_BxS2_bk0 = _rec_inputs()

    def _L0_attn_setup():
        import jax, jax.numpy as jnp
        import numpy as np
        B, N, H = (2, 1024, 512)
        NH, HD = (16, 128)
        BLK = 64
        EPS = 1e-06

        def _lightning_attn(x, slope_rate, w_qkv, w_gate, w_out, norm_w):
            b, n, _ = x.shape
            h, d = (NH, HD)
            nb = n // BLK
            qkv = jax.nn.silu(jnp.einsum('bnf,of->bno', x, w_qkv))
            qkv = qkv.reshape(b, n, h, 3 * d)
            q, k, v = jnp.split(qkv, 3, axis=-1)
            q = q.transpose(0, 2, 1, 3)
            k = k.transpose(0, 2, 1, 3)
            v = v.transpose(0, 2, 1, 3)
            s = slope_rate.astype(jnp.float32)
            arr = jnp.arange(1, BLK + 1, dtype=jnp.float32)
            q_decay = jnp.exp(-s * arr[:, None])
            k_decay = jnp.exp(-s * (BLK - arr)[:, None])
            idx = arr[:, None] - arr[None, :]
            diag_decay = jnp.where(idx >= 0, jnp.exp(-s * idx), 0.0)
            block_decay = jnp.exp(-s * BLK)
            qb = q.reshape(b, h, nb, BLK, d).transpose(2, 0, 1, 3, 4)
            kb = k.reshape(b, h, nb, BLK, d).transpose(2, 0, 1, 3, 4)
            vb = v.reshape(b, h, nb, BLK, d).transpose(2, 0, 1, 3, 4)

            def step(kv, blk):
                qi, ki, vi = blk
                o_inter = jnp.einsum('bhmd,bhde->bhme', qi * q_decay, kv)
                qk = jnp.einsum('bhmd,bhnd->bhmn', qi, ki) * diag_decay
                o_intra = jnp.einsum('bhmn,bhne->bhme', qk, vi)
                kv_new = block_decay * kv + jnp.einsum('bhmd,bhme->bhde', ki * k_decay, vi)
                return (kv_new, o_inter + o_intra)
            kv0 = jnp.zeros((b, h, d, d), dtype=jnp.float32)
            _, out = jax.lax.scan(step, kv0, (qb, kb, vb))
            out = out.transpose(1, 2, 0, 3, 4).reshape(b, h, n, d)
            out = out.transpose(0, 2, 1, 3).reshape(b, n, h * d)
            var = jnp.mean(out * out, axis=-1, keepdims=True)
            out = norm_w * (out * jax.lax.rsqrt(var + EPS))
            gate = jax.nn.sigmoid(jnp.einsum('bnf,of->bno', x, w_gate))
            return jnp.einsum('bno,fo->bnf', gate * out, w_out)
        key = jax.random.key(seed)
        ks = jax.random.split(key, 5)
        scale = 0.02
        x = jax.random.normal(ks[0], (B, N, H), dtype=jnp.float32)
        slopes = (1.0 / 2.0 ** (8.0 * np.arange(1, NH + 1) / NH)).astype(np.float32)
        slope_rate = jnp.asarray(slopes).reshape(NH, 1, 1)
        w_qkv = jax.random.normal(ks[1], (3 * NH * HD, H), dtype=jnp.float32) * scale
        w_gate = jax.random.normal(ks[2], (NH * HD, H), dtype=jnp.float32) * scale
        w_out = jax.random.normal(ks[3], (H, NH * HD), dtype=jnp.float32) * scale
        norm_w = jnp.ones((NH * HD,), dtype=jnp.float32)
        return {'hidden_states': x, 'slope_rate': slope_rate, 'w_qkv': w_qkv, 'w_gate': w_gate, 'w_out': w_out, 'norm_w': norm_w}
    _L0_attn_all = _L0_attn_setup()
    _L0_attn_in = {k: v for k, v in _L0_attn_all.items() if k in ('slope_rate', 'w_qkv', 'w_gate', 'w_out', 'norm_w')}
    del _L0_attn_all

    def _L0_xattn_setup():
        import jax, jax.numpy as jnp
        import numpy as np
        key = jax.random.key(seed)
        k1, k2, k3 = jax.random.split(key, 3)
        B, S, D, M = (8, 512, 512, 128)
        hidden_states = jax.random.normal(k1, (B, S, D), dtype=jnp.float32)
        memory_tokens = jax.random.normal(k2, (B, M, D), dtype=jnp.float32)
        memory_mask = jax.random.randint(k3, (B, M), 0, 2).astype(jnp.bool_)
        return {'hidden_states': hidden_states, 'memory_tokens': memory_tokens, 'memory_mask': memory_mask}
    _L0_xattn_all = _L0_xattn_setup()
    _L0_xattn_in = {k: v for k, v in _L0_xattn_all.items() if k in ()}
    del _L0_xattn_all

    def _L0_ffn_setup():
        import jax, jax.numpy as jnp
        import numpy as np
        FP8_MAX = 448.0
        GLOBAL_DIV = 448.0 * 6.0

        def _fp8(x):
            return x.astype(jnp.float8_e4m3fn).astype(jnp.float32)

        def _reorder_quantize_x(x, idx):
            scale = jnp.max(jnp.abs(x)) / GLOBAL_DIV
            xr = (x / scale)[:, idx]
            scale_x = jnp.max(jnp.abs(xr), axis=1, keepdims=True) / FP8_MAX
            qx = _fp8(xr / scale_x)
            return (qx, scale_x, scale)

        def _qlinear(qx, scale_x, scale, W, idx, out_idx=None):
            Wr = W[:, idx]
            w_scale = jnp.max(jnp.abs(Wr), axis=1, keepdims=True) / FP8_MAX
            qw = _fp8(Wr / w_scale)
            y = qx * scale_x @ (qw * w_scale).T * scale
            if out_idx is not None:
                y = y[:, out_idx]
            return y
        key = jax.random.key(seed)
        ks = jax.random.split(key, 6)
        B, S, H, I = (2, 256, 512, 1408)
        return {'x': jax.random.normal(ks[0], (B, S, H), jnp.float32), 'w_gate': jax.random.normal(ks[1], (I, H), jnp.float32) * 0.02, 'w_up': jax.random.normal(ks[2], (I, H), jnp.float32) * 0.02, 'w_down': jax.random.normal(ks[3], (H, I), jnp.float32) * 0.02, 'up_reorder_index': jax.random.permutation(ks[4], jnp.arange(H, dtype=jnp.int64)), 'down_reorder_index': jax.random.permutation(ks[5], jnp.arange(I, dtype=jnp.int64))}
    _L0_ffn_all = _L0_ffn_setup()
    _L0_ffn_in = {k: v for k, v in _L0_ffn_all.items() if k in ('w_gate', 'w_up', 'w_down', 'up_reorder_index', 'down_reorder_index')}
    del _L0_ffn_all
    return {'x': x, 'ctx_2048': ctx_2048, 'mask_BxS2_bk0': mask_BxS2_bk0, 'L0_attn_slope_rate': _L0_attn_in['slope_rate'], 'L0_attn_w_qkv': _L0_attn_in['w_qkv'], 'L0_attn_w_gate': _L0_attn_in['w_gate'], 'L0_attn_w_out': _L0_attn_in['w_out'], 'L0_attn_norm_w': _L0_attn_in['norm_w'], 'L0_ffn_w_gate': _L0_ffn_in['w_gate'], 'L0_ffn_w_up': _L0_ffn_in['w_up'], 'L0_ffn_w_down': _L0_ffn_in['w_down'], 'L0_ffn_up_reorder_index': _L0_ffn_in['up_reorder_index'], 'L0_ffn_down_reorder_index': _L0_ffn_in['down_reorder_index']}

def reference(x, ctx_2048, mask_BxS2_bk0, L0_attn_slope_rate, L0_attn_w_qkv, L0_attn_w_gate, L0_attn_w_out, L0_attn_norm_w, L0_ffn_w_gate, L0_ffn_w_up, L0_ffn_w_down, L0_ffn_up_reorder_index, L0_ffn_down_reorder_index):
    import jax
    import jax.numpy as jnp

    def _L0_attn_ref(hidden_states, slope_rate, w_qkv, w_gate, w_out, norm_w):
        import jax, jax.numpy as jnp
        import numpy as np
        B, N, H = (2, 1024, 512)
        NH, HD = (16, 128)
        BLK = 64
        EPS = 1e-06

        def _lightning_attn(x, slope_rate, w_qkv, w_gate, w_out, norm_w):
            b, n, _ = x.shape
            h, d = (NH, HD)
            nb = n // BLK
            qkv = jax.nn.silu(jnp.einsum('bnf,of->bno', x, w_qkv))
            qkv = qkv.reshape(b, n, h, 3 * d)
            q, k, v = jnp.split(qkv, 3, axis=-1)
            q = q.transpose(0, 2, 1, 3)
            k = k.transpose(0, 2, 1, 3)
            v = v.transpose(0, 2, 1, 3)
            s = slope_rate.astype(jnp.float32)
            arr = jnp.arange(1, BLK + 1, dtype=jnp.float32)
            q_decay = jnp.exp(-s * arr[:, None])
            k_decay = jnp.exp(-s * (BLK - arr)[:, None])
            idx = arr[:, None] - arr[None, :]
            diag_decay = jnp.where(idx >= 0, jnp.exp(-s * idx), 0.0)
            block_decay = jnp.exp(-s * BLK)
            qb = q.reshape(b, h, nb, BLK, d).transpose(2, 0, 1, 3, 4)
            kb = k.reshape(b, h, nb, BLK, d).transpose(2, 0, 1, 3, 4)
            vb = v.reshape(b, h, nb, BLK, d).transpose(2, 0, 1, 3, 4)

            def step(kv, blk):
                qi, ki, vi = blk
                o_inter = jnp.einsum('bhmd,bhde->bhme', qi * q_decay, kv)
                qk = jnp.einsum('bhmd,bhnd->bhmn', qi, ki) * diag_decay
                o_intra = jnp.einsum('bhmn,bhne->bhme', qk, vi)
                kv_new = block_decay * kv + jnp.einsum('bhmd,bhme->bhde', ki * k_decay, vi)
                return (kv_new, o_inter + o_intra)
            kv0 = jnp.zeros((b, h, d, d), dtype=jnp.float32)
            _, out = jax.lax.scan(step, kv0, (qb, kb, vb))
            out = out.transpose(1, 2, 0, 3, 4).reshape(b, h, n, d)
            out = out.transpose(0, 2, 1, 3).reshape(b, n, h * d)
            var = jnp.mean(out * out, axis=-1, keepdims=True)
            out = norm_w * (out * jax.lax.rsqrt(var + EPS))
            gate = jax.nn.sigmoid(jnp.einsum('bnf,of->bno', x, w_gate))
            return jnp.einsum('bno,fo->bnf', gate * out, w_out)
        return _lightning_attn(hidden_states, slope_rate, w_qkv, w_gate, w_out, norm_w)

    def _L0_xattn_ref(hidden_states, memory_tokens, memory_mask):
        import jax, jax.numpy as jnp
        import numpy as np
        B, S, D = hidden_states.shape
        scale = 1.0 / jnp.sqrt(jnp.asarray(D, hidden_states.dtype))
        scores = jnp.einsum('bsd,bmd->bsm', hidden_states, memory_tokens) * scale
        neg_inf = jnp.asarray(-1e+30, scores.dtype)
        scores = jnp.where(memory_mask[:, None, :], scores, neg_inf)
        attn = jax.nn.softmax(scores, axis=-1)
        readout = jnp.einsum('bsm,bmd->bsd', attn, memory_tokens)
        valid_b = jnp.any(memory_mask, axis=-1)
        out = jnp.where(valid_b[:, None, None], readout, jnp.zeros_like(readout))
        return out

    def _L0_ffn_ref(x, w_gate, w_up, w_down, up_reorder_index, down_reorder_index):
        import jax, jax.numpy as jnp
        import numpy as np
        FP8_MAX = 448.0
        GLOBAL_DIV = 448.0 * 6.0

        def _fp8(x):
            return x.astype(jnp.float8_e4m3fn).astype(jnp.float32)

        def _reorder_quantize_x(x, idx):
            scale = jnp.max(jnp.abs(x)) / GLOBAL_DIV
            xr = (x / scale)[:, idx]
            scale_x = jnp.max(jnp.abs(xr), axis=1, keepdims=True) / FP8_MAX
            qx = _fp8(xr / scale_x)
            return (qx, scale_x, scale)

        def _qlinear(qx, scale_x, scale, W, idx, out_idx=None):
            Wr = W[:, idx]
            w_scale = jnp.max(jnp.abs(Wr), axis=1, keepdims=True) / FP8_MAX
            qw = _fp8(Wr / w_scale)
            y = qx * scale_x @ (qw * w_scale).T * scale
            if out_idx is not None:
                y = y[:, out_idx]
            return y
        B, S, H = x.shape
        xf = x.reshape(B * S, H)
        qx, sx, sc = _reorder_quantize_x(xf, up_reorder_index)
        g = _qlinear(qx, sx, sc, w_gate, up_reorder_index, out_idx=down_reorder_index)
        u = _qlinear(qx, sx, sc, w_up, up_reorder_index, out_idx=down_reorder_index)
        t = jax.nn.silu(g) * u
        qt, st, sct = _reorder_quantize_x(t, down_reorder_index)
        y = _qlinear(qt, st, sct, w_down, down_reorder_index)
        return y.reshape(B, S, H)
    x = x + _L0_attn_ref(_layernorm(x, axis=-1), L0_attn_slope_rate, L0_attn_w_qkv, L0_attn_w_gate, L0_attn_w_out, L0_attn_norm_w)
    x = x + _L0_xattn_ref(_layernorm(x, axis=-1), ctx_2048, mask_BxS2_bk0)
    x = x + _L0_ffn_ref(_layernorm(x, axis=-1), L0_ffn_w_gate, L0_ffn_w_up, L0_ffn_w_down, L0_ffn_up_reorder_index, L0_ffn_down_reorder_index)
    return x

_drawn_inputs = setup_inputs


def setup_inputs(seed=0):
    import zlib

    import numpy as np

    out = dict(_drawn_inputs(seed))
    spreads = {'L0_attn_norm_w': (1.0, 0.2)}
    factors = {}
    for name, (base, spread) in spreads.items():
        noise = np.random.default_rng([zlib.crc32(name.encode()), seed]).standard_normal(out[name].shape)
        drawn = base * np.exp(spread * noise) if base else spread * noise
        out[name] = jnp.asarray(drawn.astype(out[name].dtype))
    for name, factor in factors.items():
        out[name] = (out[name] * factor).astype(out[name].dtype)
    return out
```

```python
from contextlib import ExitStack

import numpy as np

import concourse.bass as bass
from concourse import mybir

P = 128
ALU = mybir.AluOpType
ACT = mybir.ActivationFunctionType
AX = mybir.AxisListType.X
F32 = mybir.dt.float32
F32R = mybir.dt.float32r
F16 = mybir.dt.float16
I32 = mybir.dt.int32
U32 = mybir.dt.uint32
U8 = mybir.dt.uint8

LN_EPS = 1e-5
RMS_EPS = 1e-6
NEG = 1e30
EXPONENT_BITS = 0x7F800000
TOP_MANTISSA_BIT = 0x00400000
FP8_MAX = 448.0


class Steps:

    def __init__(self, sem, base=0):
        self.sem, self.base, self.n = sem, base, 0

    def did(self, ins):
        ins.then_inc(self.sem, 1)
        self.n += 1
        return ins

    def wait(self, eng, back=0):
        eng.wait_ge(self.sem, self.base + (self.n - back))


def rsqrt(eng, st, out, x, tmp, tmp2, mean_of, eps):
    st.wait(eng)
    st.did(eng.tensor_scalar(x, x, 1.0 / mean_of, eps, ALU.mult, ALU.add))
    st.wait(eng)
    st.did(eng.tensor_scalar(tmp.bitcast(U32), x.bitcast(U32), 1, None, ALU.logical_shift_right))
    st.wait(eng)
    st.did(eng.tensor_scalar(out.bitcast(I32), tmp.bitcast(I32), -1.0, float(0x5F3759DF), ALU.mult, ALU.add))
    for _ in range(4):
        st.wait(eng)
        st.did(eng.tensor_tensor(tmp, out, out, ALU.mult))
        st.wait(eng)
        st.did(eng.tensor_tensor(tmp2, tmp, x, ALU.mult))
        st.wait(eng)
        st.did(eng.tensor_scalar(tmp, tmp2, -0.5, 1.5, ALU.mult, ALU.add))
        st.wait(eng)
        st.did(eng.tensor_tensor(out, out, tmp, ALU.mult))


def round_fp8(eng, st, v, mag, q):
    st.wait(eng)
    st.did(eng.tensor_scalar(mag.bitcast(U32), v.bitcast(U32), EXPONENT_BITS, TOP_MANTISSA_BIT,
                             ALU.bitwise_and, ALU.bitwise_or))
    st.wait(eng)
    st.did(eng.tensor_scalar(mag, mag, 1.5 * 2.0 ** -6, 2.0 ** 20, ALU.max, ALU.mult))
    st.wait(eng)
    st.did(eng.tensor_tensor(v, v, mag, ALU.add))
    st.wait(eng)
    st.did(eng.tensor_tensor(q, v, mag, ALU.subtract))


def layer(nc, x, ctx, ctx_t, pad_mask, slope, w_qkv1, w_qkv2, w_gate, w_out, norm_w, f_gate, f_up, f_down,
          up_idx, down_idx, out):
    B, S, D = x.shape
    NH = slope.shape[1]
    decay_dram = nc.dram_tensor("decay_tables", [NH, P, S], F32, kind="Internal").ap()
    x1_dram = nc.dram_tensor("after_attention", [B, S, D], F32, kind="Internal").ap()
    with ExitStack() as top:
        c = Shared()
        c.ident = top.enter_context(nc.sbuf_tensor("ident", [P, P], F32))
        c.ident16 = top.enter_context(nc.sbuf_tensor("ident16", [P, P], F16))
        c.ones = top.enter_context(nc.sbuf_tensor("ones", [P, P], F32))
        c.zeros = top.enter_context(nc.sbuf_tensor("zeros", [P, 512], F16))
        c.bank = [top.enter_context(nc.psum_tensor(f"bank{i}", [P, 512], F32)) for i in range(8)]
        constants(nc, c, slope, decay_dram)
        attention(nc, c, x, w_qkv1, w_qkv2, w_gate, w_out, norm_w, decay_dram, x1_dram)
        F = f_gate.shape[0]
        c.gateT = top.enter_context(nc.sbuf_tensor("gateT", [P, D // P, F], F16))
        c.upT = top.enter_context(nc.sbuf_tensor("upT", [P, D // P, F], F16))
        c.downT = top.enter_context(nc.sbuf_tensor("downT", [P, F // P, D], F16))
        c.gate_sc = top.enter_context(nc.sbuf_tensor("gate_sc", [P, F], F32))
        c.up_sc = top.enter_context(nc.sbuf_tensor("up_sc", [P, F], F32))
        c.down_sc = top.enter_context(nc.sbuf_tensor("down_sc", [P, D], F32))
        c.up_named = top.enter_context(nc.sbuf_tensor("up_named", [P, D], F32))
        c.down_named = top.enter_context(nc.sbuf_tensor("down_named", [P, F], F32))
        ffn_weights(nc, c, f_gate, f_up, f_down, up_idx, down_idx)
        tail(nc, c, ctx, ctx_t, pad_mask, x1_dram, out)


class Shared:
    pass


def spans(F):
    return [(a, min(512, F - a)) for a in range(0, F, 512)]


def scope(nc, stage):
    c = ExitStack()
    return (c, lambda name, shape, dt=F32: c.enter_context(nc.sbuf_tensor(f"{stage}_{name}", shape, dt)),
            lambda name: c.enter_context(nc.semaphore(f"{stage}_{name}")))


def prime(nc, semaphores):
    with nc.Block() as block:
        @block.sync
        def _(sp):
            for s in semaphores:
                sp.sem_inc(s, 1)


def constants(nc, c, slope, decay_dram):
    NH, _, S = decay_dram.shape
    ctx, sb, sem = scope(nc, "constants")
    with ctx:
        dist_i = sb("dist_i", [P, S], I32)
        dist = sb("dist", [P, S])
        tri = sb("tri", [P, S])
        slope_b = sb("slope_b", [P, NH])
        dec_e = sb("dec_e", [P, 2, S])
        dec = sb("dec", [P, 2, S])
        s_pool = sem("pool_constants")
        s_in = sem("slope_landed")
        s_dv = sem("dve_constants")
        s_exp = sem("table_exp")
        s_dec = sem("table_ready")
        s_decout = [sem("tables0_stored"), sem("tables1_stored")]
        with nc.Block() as block:
            @block.gpsimd
            def _(g):
                g.memset(c.zeros[:, :], 0.0).then_inc(s_pool, 1)
                g.memset(c.ident[:, :], 0.0).then_inc(s_pool, 1)
                g.memset(c.ones[:, :], 1.0).then_inc(s_pool, 1)
                g.memset(tri[:, :], 1.0).then_inc(s_pool, 1)
                g.iota(dist_i[:, :], [[1, S]], base=0, channel_multiplier=-1).then_inc(s_pool, 1)
                g.wait_ge(s_pool, 5)
                g.affine_select(out=c.ident[:, :], in_=c.ident[:, :], compare_op=ALU.not_equal, fill=1.0,
                                base=0, pattern=[[-1, P]], channel_multiplier=1).then_inc(s_pool, 1)
                g.affine_select(out=tri[:, :], in_=tri[:, :], compare_op=ALU.is_ge, fill=0.0,
                                base=0, pattern=[[1, S]], channel_multiplier=-1).then_inc(s_pool, 1)

            @block.sync
            def _(sp):
                sp.dma_start(slope_b[:, :], slope.to_broadcast([P, NH])).then_inc(s_in, 16)
                for h in range(NH):
                    sp.wait_ge(s_dec, h + 1)
                    sp.dma_start(decay_dram[h], dec[:, h % 2, :]).then_inc(s_decout[h % 2], 16)
                for q in s_decout:
                    sp.wait_ge(q, 16 * NH // 2)

            @block.scalar
            def _(act):
                act.wait_ge(s_dv, 4)
                for h in range(NH):
                    if h >= 2:
                        act.wait_ge(s_dec, h - 1)
                    nc.scalar.activation(dec_e[:, h % 2, :], dist[:, :], ACT.Exp,
                                         scale=slope_b[:, h:h + 1]).then_inc(s_exp, 1)

            @block.vector
            def _(v):
                v.wait_ge(s_pool, 7)
                v.tensor_copy(c.ident16[:, :], c.ident[:, :]).then_inc(s_dv, 1)
                v.tensor_copy(dist[:, :], dist_i[:, :]).then_inc(s_dv, 1)
                v.wait_ge(s_dv, 2)
                v.tensor_scalar(dist[:, :], dist[:, :], 0.0, None, ALU.max).then_inc(s_dv, 1)
                v.wait_ge(s_in, 16)
                v.tensor_scalar(slope_b[:, :], slope_b[:, :], -1.0, None, ALU.mult).then_inc(s_dv, 1)
                for h in range(NH):
                    v.wait_ge(s_exp, h + 1)
                    if h >= 2:
                        v.wait_ge(s_decout[h % 2], 16 * (h // 2))
                    v.tensor_tensor(dec[:, h % 2, :], dec_e[:, h % 2, :], tri[:, :], ALU.mult).then_inc(s_dec, 1)


def ffn_weights(nc, c, f_gate, f_up, f_down, up_idx, down_idx):
    F, D = f_gate.shape
    KD, KF = D // P, F // P
    FS = spans(F)
    ident, ident16, bank = c.ident, c.ident16, c.bank
    tasks = [("g", t) for t in range(KF)] + [("u", t) for t in range(KF)] + [("d", t) for t in range(KD)]
    ctx, sb, sem = scope(nc, "ffn_weights")
    with ctx:
        col_i = sb("col_i", [P, F], I32)
        col = sb("col", [P, F])
        uix, dix = sb("uix", [P, KD], I32), sb("dix", [P, KF], I32)
        uixf, dixf = sb("uixf", [P, KD]), sb("dixf", [P, KF])
        hot = sb("hot", [P, 2, F], F16)
        ones16 = sb("ones16", [P, P], F16)
        up_cnt, down_cnt = sb("up_cnt", [P, D]), sb("down_cnt", [P, F])
        rows = sb("rows", [P, 2, F])
        w_v, w_mag = sb("w_v", [P, F]), sb("w_mag", [P, F])
        w_q = sb("w_q", [P, F], F16)
        w_s = sb("w_s", [P, 4])
        diag = sb("diag", [P, P])
        s_pool = sem("pool_iota")
        s_ix = sem("indices_landed")
        s_dv = sem("weight_steps")
        s_hot = sem("one_hot_ready")
        s_cnt = sem("counts_summed")
        s_rows = [sem("rows0_landed"), sem("rows1_landed")]
        s_used = sem("rows_used")
        s_quant = sem("rows_quantised")
        s_tr = sem("rows_turned")
        s_spread = sem("scales_spread")
        s_evac = sem("turned_copied")
        with nc.Block() as block:
            @block.gpsimd
            def _(g):
                g.memset(ones16[:, :], 1.0).then_inc(s_pool, 1)
                g.iota(col_i[:, :], [[1, F]], base=0, channel_multiplier=0).then_inc(s_pool, 1)
                g.wait_ge(s_ix, 32)
                for n, (kind, t) in enumerate(tasks):
                    if n >= 2:
                        g.wait_ge(s_used, n - 1)
                    if kind == "d":
                        g.dma_start(rows[:, n % 2, :], f_down[t * P:(t + 1) * P, :]).then_inc(s_rows[n % 2], 16)
                    else:
                        g.indirect_dma_start(rows[:, n % 2, 0:D], None, f_gate if kind == "g" else f_up,
                                             bass.IndirectOffsetOnAxis(ap=dix[:, t:t + 1], axis=0)
                                             ).then_inc(s_rows[n % 2], 16)

            @block.sync
            def _(sp):
                sp.dma_start(uix[:, :], up_idx).then_inc(s_ix, 16)
                sp.dma_start(dix[:, :], down_idx).then_inc(s_ix, 16)

            @block.scalar
            def _(act):
                for n, (kind, t) in enumerate(tasks):
                    dst = {"g": c.gateT, "u": c.upT, "d": c.downT}[kind]
                    nb = KF if kind == "d" else KD
                    act.wait_ge(s_tr, n + 1)
                    for half in range(0, nb, 8):
                        k = min(8, nb - half)
                        ins = nc.scalar.copy(dst[:, half:half + k, t * P:(t + 1) * P],
                                             bank[1 + half // 8][:, 0:k * P // 2].bitcast(F16)
                                             .rearrange("p (k i) -> p k i", i=P))
                    ins.then_inc(s_evac, 1)

            @block.tensor
            def _(pe):
                pe.wait_ge(s_pool, 2)
                for n in range(KD):
                    pe.wait_ge(s_hot, n + 1)
                    pe.matmul(bank[3][:, 0:D], ones16[:, :], hot[:, n % 2, 0:D], start=(n == 0),
                              stop=(n == KD - 1)).then_inc(s_cnt, 1)
                for n in range(KF):
                    pe.wait_ge(s_hot, KD + n + 1)
                    for i, (a, w) in enumerate(FS):
                        mm = pe.matmul(bank[4 + i][:, 0:w], ones16[:, :], hot[:, (KD + n) % 2, a:a + w],
                                       start=(n == 0), stop=(n == KF - 1))
                    mm.then_inc(s_cnt, 1)
                for n, (kind, t) in enumerate(tasks):
                    pe.wait_ge(s_quant, n + 1)
                    if n:
                        pe.wait_ge(s_evac, n)
                    for k in range(KF if kind == "d" else KD):
                        mm = pe.transpose(bank[1 + k // 8][:, (k % 8) * 64:(k % 8 + 1) * 64].bitcast(F16),
                                          w_q[:, k * P:(k + 1) * P], ident16[:, :])
                    mm.then_inc(s_tr, 1)
                    pe.matmul(bank[0][:, 0:P], c.ones[:, :], diag[:, :], start=True, stop=True).then_inc(s_spread, 1)

            @block.vector
            def _(v):
                st = Steps(s_dv)
                v.wait_ge(s_pool, 2)
                st.did(v.tensor_copy(col[:, :], col_i[:, :]))
                v.wait_ge(s_ix, 32)
                st.did(v.tensor_copy(uixf[:, :], uix[:, :]))
                st.did(v.tensor_copy(dixf[:, :], dix[:, :]))
                st.wait(v)
                for n in range(KD + KF):
                    if n >= 2:
                        v.wait_ge(s_cnt, n - 1)
                    w, ix = (D, uixf[:, n:n + 1]) if n < KD else (F, dixf[:, n - KD:n - KD + 1])
                    v.tensor_scalar(hot[:, n % 2, 0:w], col[:, 0:w], ix, None, ALU.is_equal).then_inc(s_hot, 1)
                v.wait_ge(s_cnt, KD + KF)
                for named, cnt, parts in ((c.up_named, up_cnt, [(3, 0, D)]),
                                          (c.down_named, down_cnt, [(4 + i, a, w) for i, (a, w) in enumerate(FS)])):
                    for b, a, w in parts:
                        st.did(v.tensor_scalar(named[:, a:a + w], bank[b][:, 0:w], 1.0, None, ALU.min))
                        st.did(v.tensor_scalar(cnt[:, a:a + w], bank[b][:, 0:w], 0.25, None, ALU.mult))
                for n, (kind, t) in enumerate(tasks):
                    w = F if kind == "d" else D
                    named, cnt = (c.down_named, down_cnt) if kind == "d" else (c.up_named, up_cnt)
                    wv, r = w_v[:, 0:w], rows[:, n % 2, 0:w]
                    v.wait_ge(s_rows[n % 2], 16 * (n // 2 + 1))
                    st.wait(v)
                    v.tensor_tensor(wv, r, named[:, 0:w], ALU.mult).then_inc(s_used, 1)
                    v.wait_ge(s_used, n + 1)
                    st.did(v.tensor_reduce(w_s[:, 0:1], wv, AX, ALU.max, apply_absolute_value=True))
                    st.wait(v)
                    st.did(v.tensor_scalar(w_s[:, 1:2], w_s[:, 0:1], 1.0 / FP8_MAX, None, ALU.mult))
                    st.wait(v)
                    st.did(v.reciprocal(w_s[:, 2:3], w_s[:, 1:2]))
                    st.wait(v)
                    st.did(v.tensor_scalar(wv, wv, w_s[:, 2:3], None, ALU.mult))
                    round_fp8(v, st, wv, w_mag[:, 0:w], wv)
                    if n:
                        v.wait_ge(s_spread, n)
                    st.did(v.tensor_scalar(diag[:, :], ident[:, :], w_s[:, 1:2], None, ALU.mult))
                    st.wait(v)
                    v.tensor_tensor(w_q[:, 0:w], wv, cnt[:, 0:w], ALU.mult).then_inc(s_quant, 1)
                    v.wait_ge(s_spread, n + 1)
                    dst = {"g": c.gate_sc, "u": c.up_sc, "d": c.down_sc}[kind]
                    st.did(v.tensor_copy(dst[:, t * P:(t + 1) * P], bank[0][:, 0:P]))


def attention(nc, c, x, w_qkv1, w_qkv2, w_gate, w_out, norm_w, decay_dram, x1_dram):
    B, S, D = x.shape
    NH = decay_dram.shape[0]
    KD, KT, NP = D // P, S // P, NH // 2
    assert KD == 4 and KT == 4
    ident, bank = c.ident, c.bank
    ctx, sb, sem = scope(nc, "attention")
    with ctx:
        x_in, normed = sb("x_in", [P, KT, D]), sb("normed", [P, KT, D])
        x_res, x1 = sb("x_res", [P, KT, D]), sb("x1", [P, KT, D])
        stats, mv = sb("stats", [P, KT, 6]), sb("mv", [P, KT, 2])
        sm = sb("sm", [P, 8, KT])
        xTh, xTl = sb("xTh", [P, KD, S], F32R), sb("xTl", [P, KD, S], F32R)
        WN = [KD * 4 * P, KD * 2 * P, KD * 2 * P, 2 * D]
        raw = [sb(f"raw{i}", [P, n]) for i, n in enumerate(WN)]
        wh = [sb(f"w_hi{i}", [P, n], F32R) for i, n in enumerate(WN)]
        wl = [sb(f"w_lo{i}", [P, n], F32R) for i, n in enumerate(WN)]
        w_src = [w_qkv1, w_qkv2, w_gate, w_out]
        nw = sb("nw", [P, NH])
        dcy = sb("dcy", [P, 2, S])
        sig_q, sig_k, sig_v = sb("sig_q", [P, S]), sb("sig_k", [P, S]), sb("sig_v", [P, KT, 2 * P])
        qf, kf, vf = sb("qf", [P, S]), sb("kf", [P, S]), sb("vf", [P, KT, 2 * P])
        qh, ql = sb("qh", [P, S], F32R), sb("ql", [P, S], F32R)
        kh, kl = sb("kh", [P, S], F32R), sb("kl", [P, S], F32R)
        vh, vl = sb("vh", [P, KT, 2 * P], F32R), sb("vl", [P, KT, 2 * P], F32R)
        Q0 = [0, 128, 256, 256]
        OFF = [0, 512, 896, 1152, 1408]
        sf = sb("sf", [P, OFF[4]])
        sh, sl = sb("sh", [P, OFF[4]], F32R), sb("sl", [P, OFF[4]], F32R)
        gate, of, og = sb("gate", [P, S]), sb("of", [P, S]), sb("og", [P, S])
        ogh, ogl = sb("ogh", [P, S], F32R), sb("ogl", [P, S], F32R)
        sq, sq_sum = sb("sq", [P, S]), sb("sq_sum", [P, S])
        W, Y = bank[0:4], bank[4:8]
        part = [[t.rearrange("p (k c) -> p k c", k=k) for t, k in zip(ws, (KD, KD, KD, 2))] for ws in
                ([w[:, :] for w in wh], [w[:, :] for w in wl])]

        s_x, s_xres, s_nw = sem("x_landed"), sem("x_res_landed"), sem("norm_w_landed")
        s_raw = [sem(f"raw{i}_landed") for i in range(4)]
        s_wh = [sem(f"w{i}_hi_ready") for i in range(4)]
        s_wl = [sem(f"w{i}_lo_ready") for i in range(4)]
        s_dcy = [sem(f"decay{i}_landed") for i in range(2)]
        s_ln, s_normed, s_xt = sem("norm_steps"), sem("normed_ready"), sem("x_turned")
        s_xh, s_xl = sem("x_hi_ready"), sem("x_lo_ready")
        s_q, s_k, s_v = sem("q_summed"), sem("k_summed"), sem("v_summed")
        s_s, s_g, s_o, s_op = sem("scores_summed"), sem("gate_summed"), sem("o_summed"), sem("y_added")
        s_sigq, s_sigk, s_sigv = sem("q_sigmoid"), sem("k_sigmoid"), sem("v_sigmoid")
        s_qm, s_km, s_vm = sem("q_ready"), sem("k_ready"), sem("v_ready")
        s_qh, s_kh, s_vh = sem("q_hi_ready"), sem("k_hi_ready"), sem("v_hi_ready")
        s_ql, s_kl, s_vl = sem("q_lo_ready"), sem("k_lo_ready"), sem("v_lo_ready")
        s_mask = [sem("scores_decayed0"), sem("scores_decayed1")]
        s_sh, s_sl = sem("scores_hi_ready"), sem("scores_lo_ready")
        s_gate, s_of, s_og = sem("gate_ready"), sem("o_copied"), sem("gated")
        s_ogh, s_ogl = sem("gated_hi_ready"), sem("gated_lo_ready")
        s_sq, s_acc, s_zero = sem("o_squared"), sem("squares_added"), sem("squares_cleared")
        s_ssum, s_fin = sem("squares_summed"), sem("batch_end_steps")
        s_x1, s_x1out = sem("x1_ready"), sem("x1_stored")
        LN_STEPS, FIN_STEPS = 2 * KT + 2 + 19, 1 + 19

        prime(nc, [s_normed, *s_wh, *s_wl, *s_mask, s_x1, s_ssum, s_op, s_acc, s_qm, s_km, s_vm, s_o, s_og, s_sq, s_of,
                   s_gate, s_ogl, s_x1out, s_xt, s_ln])
        PASSES = [(0, 0), (0, 1), (1, 0)]

        with nc.Block() as block:
            @block.sync
            def _(sp):
                def load(i, p, n):
                    sp.wait_ge(s_wh[i], n + 1)
                    sp.wait_ge(s_wl[i], n + 1)
                    sp.dma_start(raw[i][:, :], w_src[i][p]).then_inc(s_raw[i], 16)

                sp.dma_start(nw[:, :], norm_w).then_inc(s_nw, 16)
                with sp.Fori(0, B) as b:
                    sp.wait_ge(s_normed, KT * b + 1)
                    sp.dma_start(x_in[:, :, :], x[b].rearrange("(t p) d -> p t d", p=P)).then_inc(s_x, 16)
                    with sp.Fori(0, NP) as p:
                        n = b * NP + p
                        for i in range(4):
                            load(i, p, n)
                        for j in range(2):
                            sp.wait_ge(s_mask[j], n * 3 + 1)
                            sp.dma_start(dcy[:, j, :], decay_dram[p * 2 + j]).then_inc(s_dcy[j], 16)
                for i in range(3):
                    load(i, 0, B * NP)

            @block.gpsimd
            def _(g):
                def weights_lo(i, n):
                    g.wait_ge(s_wh[i], n + 1 + 1)
                    g.tensor_tensor(wl[i][:, :], raw[i][:, :], wh[i][:, :].bitcast(F32), ALU.subtract).then_inc(s_wl[i], 1)

                def slot(pair, j, b):
                    n = pair * 2 + j
                    if j == 0:
                        weights_lo(3, pair)
                    g.wait_ge(s_acc, n + 1)
                    g.wait_ge(s_of, n + 1 + 1)
                    g.tensor_tensor(sq[:, :], of[:, :], of[:, :], ALU.mult).then_inc(s_sq, 1)
                    g.wait_ge(s_ogh, n + 1)
                    g.wait_ge(s_op, n + 1)
                    g.tensor_tensor(ogl[:, :], og[:, :], ogh[:, :].bitcast(F32), ALU.subtract).then_inc(s_ogl, 1)
                    g.wait_ge(s_sq, n + 1 + 1)
                    g.wait_ge(s_acc, n + 1)
                    g.wait_ge(s_zero, b + 1)
                    g.tensor_tensor(sq_sum[:, :], sq_sum[:, :], sq[:, :], ALU.add).then_inc(s_acc, 1)
                    for i in ((0,) if j == 0 else (2, 1)):
                        weights_lo(i, pair + 1)

                for i in range(3):
                    weights_lo(i, 0)
                with g.Fori(0, B) as b:
                    g.wait_ge(s_x1, KT * b + 1)
                    g.dma_start(x_res[:, :, :], x[b].rearrange("(t p) d -> p t d", p=P)).then_inc(s_xres, 16)
                    g.wait_ge(s_ssum, b + 1)
                    g.tensor_tensor(sq_sum[:, :], c.zeros[:, :], c.zeros[:, :], ALU.add).then_inc(s_zero, 1)
                    with g.Fori(0, NP) as p:
                        for j in range(2):
                            slot(b * NP + p, j, b)

            @block.scalar
            def _(act):
                def weights_hi(i, n):
                    act.wait_ge(s_raw[i], 16 * n + 16)
                    nc.scalar.copy(wh[i][:, :], raw[i][:, :]).then_inc(s_wh[i], 1)

                def sig(dst, src, ready, n, used, signal):
                    act.wait_ge(ready, n + 1)
                    act.wait_ge(used, n + 1)
                    nc.scalar.activation(dst, src, ACT.Sigmoid).then_inc(signal, 1)

                def sig_values(pair):
                    for i in range(2):
                        act.wait_ge(s_v, pair * 2 + i + 1)
                        act.wait_ge(s_vm, pair * 2 + 1)
                        nc.scalar.activation(sig_v[:, 2 * i:2 * i + 2, :],
                                             W[2 + i][:, :].rearrange("p (t c) -> p t c", t=2),
                                             ACT.Sigmoid).then_inc(s_sigv, 1)

                def slot(pair, j, last):
                    n = pair * 2 + j
                    for i, (a, e) in enumerate(((0, 512), (512, 896), (896, 1408))):
                        act.wait_ge(s_mask[j], pair * 3 + i + 1 + 1)
                        act.wait_ge(s_o, n + 1)
                        nc.scalar.copy(sh[:, a:e], sf[:, a:e]).then_inc(s_sh, 1)
                    sig(gate[:, :], W[3][:, :], s_g, n, s_og, s_gate)
                    if j == 0:
                        act.wait_ge(s_op, n + 1)
                        weights_hi(3, pair)
                    if not last:
                        sig(sig_q[:, :], W[0][:, :], s_q, n + 1, s_qm, s_sigq)
                    if j == 1:
                        act.wait_ge(s_g, n + 1)
                        weights_hi(2, pair + 1)
                    act.wait_ge(s_o, n + 1 + 1)
                    act.wait_ge(s_og, n + 1)
                    act.wait_ge(s_sq, n + 1)
                    nc.scalar.copy(of[:, :], W[1][:, :]).then_inc(s_of, 1)
                    if not last:
                        if j == 1:
                            sig_values(pair + 1)
                        sig(sig_k[:, :], W[0][:, :], s_k, n + 1, s_km, s_sigk)
                    if j == 0:
                        act.wait_ge(s_k, n + 1)
                        weights_hi(0, pair + 1)
                    else:
                        act.wait_ge(s_k, n + 1)
                        weights_hi(1, pair + 1)

                for i in range(3):
                    weights_hi(i, 0)
                with act.Fori(0, B) as b:
                    for k in range(KD):
                        act.wait_ge(s_xt, KD * b + k + 1 + 1)
                        nc.scalar.copy(xTh[:, k, :], W[k][:, :]).then_inc(s_xh, 1)
                    sig(sig_q[:, :], W[0][:, :], s_q, b * NH, s_qm, s_sigq)
                    sig_values(b * NP)
                    sig(sig_k[:, :], W[0][:, :], s_k, b * NH, s_km, s_sigk)
                    with act.Fori(0, NP - 1) as p:
                        for j in range(2):
                            slot(b * NP + p, j, False)
                    for j in range(2):
                        slot(b * NP + (NP - 1), j, j == 1)
                    act.wait_ge(s_x1, KT * b + KT + 1)
                    act.dma_start(x1_dram[b].rearrange("(t p) d -> p t d", p=P), x1[:, :, :]).then_inc(s_x1out, 16)
                act.wait_ge(s_x1out, 16 * B + 1)

            @block.tensor
            def _(pe):
                def head_rows(dst, i, col):
                    for k in range(KD):
                        for n, (a, b) in enumerate(PASSES):
                            mm = pe.matmul(dst, part[a][i][:, k, col:col + P], (xTh, xTl)[b][:, k, :],
                                           start=(k == 0 and n == 0), stop=(k == KD - 1 and n == 2))
                    return mm

                def wait_part(i, n):
                    pe.wait_ge(s_wh[i], n + 1 + 1)
                    pe.wait_ge(s_wl[i], n + 1 + 1)

                def values(pair):
                    for t in range(KT):
                        for k in range(KD):
                            for n, (a, b) in enumerate(PASSES):
                                mm = pe.matmul(W[2 + t // 2][:, (t % 2) * 2 * P:(t % 2 + 1) * 2 * P],
                                               (xTh, xTl)[b][:, k, t * P:(t + 1) * P],
                                               part[a][0][:, k, 2 * P:4 * P],
                                               start=(k == 0 and n == 0), stop=(k == KD - 1 and n == 2))
                        if t % 2:
                            mm.then_inc(s_v, 1)

                def slot(pair, j, last):
                    n = pair * 2 + j
                    pe.wait_ge(s_qh, n + 1)
                    pe.wait_ge(s_ql, n + 1)
                    pe.wait_ge(s_kh, n + 1)
                    pe.wait_ge(s_kl, n + 1)
                    for t in range(KT):
                        dst = W[min(t, 2)][:, (256 if t == 3 else 0):(256 if t == 3 else 0) + S - Q0[t]]
                        if t == 1:
                            pe.wait_ge(s_of, n + 1)
                        if t == 2:
                            pe.wait_ge(s_vm, pair * 2 + 2 + 1)
                        for i, (a, b) in enumerate(PASSES):
                            mm = pe.matmul(dst, (kh, kl)[a][:, t * P:(t + 1) * P], (qh, ql)[b][:, Q0[t]:S],
                                           start=(i == 0), stop=(i == 2))
                        if t != 2:
                            mm.then_inc(s_s, 1)
                    wait_part(2, pair)
                    head_rows(W[3][:, :], 2, j * P).then_inc(s_g, 1)
                    if not last:
                        wait_part(1 if j == 0 else 0, pair + j)
                        pe.wait_ge(s_mask[j], pair * 3 + 1 + 1)
                        head_rows(W[0][:, :], 1 if j == 0 else 0, 0).then_inc(s_q, 1)
                    pe.wait_ge(s_vh, pair + 1)
                    pe.wait_ge(s_vl, pair + 1)
                    pe.wait_ge(s_sh, n * 3 + 3)
                    pe.wait_ge(s_sl, n * 3 + 3)
                    for t in range(KT):
                        for i, (a, b) in enumerate(PASSES):
                            mm = pe.matmul(W[1][:, Q0[t]:S], (vh, vl)[a][:, t, j * P:(j + 1) * P],
                                           (sh, sl)[b][:, OFF[t]:OFF[t + 1]],
                                           start=(t == 0 and i == 0), stop=(t == KT - 1 and i == 2),
                                           skip_group_check=True)
                    mm.then_inc(s_o, 1)
                    if not last:
                        if j == 1:
                            pe.wait_ge(s_gate, n + 1 + 1)
                            values(pair + 1)
                        pe.wait_ge(s_qm, n + 2 + 1)
                        head_rows(W[0][:, :], 1 if j == 0 else 0, P).then_inc(s_k, 1)
                    pe.wait_ge(s_ogh, n + 1)
                    pe.wait_ge(s_ogl, n + 1 + 1)
                    wait_part(3, pair)
                    for t in range(KT):
                        for i, (a, b) in enumerate(PASSES):
                            mm = pe.matmul(Y[t][:, :], (ogh, ogl)[a][:, t * P:(t + 1) * P], part[b][3][:, j, :],
                                           start=False, stop=False, skip_group_check=True)
                    mm.then_inc(s_op, 1)

                with pe.Fori(0, B) as b:
                    pe.wait_ge(s_normed, KT * b + KT + 1)
                    pe.wait_ge(s_of, NH * b + 1)
                    pe.wait_ge(s_gate, NH * b + 1)
                    for k in range(KD):
                        for t in range(KT):
                            mm = pe.transpose(W[k][:, t * P:(t + 1) * P], normed[:, t, k * P:(k + 1) * P], ident[:, :])
                        mm.then_inc(s_xt, 1)
                    for t in range(KT):
                        pe.matmul(Y[t][:, :], c.zeros[:, 0:P], c.zeros[:, :], start=True, stop=False,
                                  skip_group_check=True)
                    pe.wait_ge(s_xh, KD * b + KD)
                    pe.wait_ge(s_xl, KD * b + KD)
                    wait_part(0, b * NP)
                    head_rows(W[0][:, :], 0, 0).then_inc(s_q, 1)
                    values(b * NP)
                    pe.wait_ge(s_qm, b * NH + 1 + 1)
                    head_rows(W[0][:, :], 0, P).then_inc(s_k, 1)
                    with pe.Fori(0, NP - 1) as p:
                        for j in range(2):
                            slot(b * NP + p, j, False)
                    for j in range(2):
                        slot(b * NP + (NP - 1), j, j == 1)
                    pe.wait_ge(s_acc, b * NH + NH + 1)
                    pe.wait_ge(s_gate, b * NH + NH + 1)
                    for t in range(KT):
                        mm = pe.matmul(W[3][:, t * P:(t + 1) * P], sq_sum[:, t * P:(t + 1) * P], c.ones[:, :],
                                       start=True, stop=True)
                    mm.then_inc(s_ssum, 1)

            @block.vector
            def _(v):
                def split(f, h, l, ready, n, hi, lo):
                    v.wait_ge(ready, n)
                    v.tensor_copy(h, f).then_inc(hi, 1)

                def silu_split(n, src, sg, f, h, l, sigd, made, hi, lo):
                    v.wait_ge(sigd, n + 1)
                    v.tensor_tensor(f[:, :], src, sg[:, :], ALU.mult).then_inc(made, 1)
                    v.wait_ge(made, n + 2)
                    v.tensor_copy(h[:, :], f[:, :]).then_inc(hi, 1)
                    v.wait_ge(hi, n + 1)
                    v.tensor_tensor(l[:, :], f[:, :], h[:, :].bitcast(F32), ALU.subtract).then_inc(lo, 1)

                def queries(n):
                    silu_split(n, W[0][:, :], sig_q, qf, qh, ql, s_sigq, s_qm, s_qh, s_ql)

                def keys(n):
                    silu_split(n, W[0][:, :], sig_k, kf, kh, kl, s_sigk, s_km, s_kh, s_kl)

                def values(pair):
                    for i in range(2):
                        v.wait_ge(s_sigv, pair * 2 + i + 1)
                        v.tensor_tensor(vf[:, 2 * i:2 * i + 2, :], W[2 + i][:, :].rearrange("p (t c) -> p t c", t=2),
                                        sig_v[:, 2 * i:2 * i + 2, :], ALU.mult).then_inc(s_vm, 1)
                    v.wait_ge(s_vm, pair * 2 + 2 + 1)
                    v.tensor_copy(vh[:, :, :], vf[:, :, :]).then_inc(s_vh, 1)
                    v.wait_ge(s_vh, pair + 1)
                    v.tensor_tensor(vl[:, :, :], vf[:, :, :], vh[:, :, :].bitcast(F32), ALU.subtract).then_inc(s_vl, 1)

                def slot(pair, j, last):
                    n = pair * 2 + j
                    v.wait_ge(s_dcy[j], pair * 16 + 16)
                    for i in range(3):
                        v.wait_ge(s_s, n * 3 + i + 1)
                        if i < 2:
                            v.tensor_tensor(sf[:, OFF[i]:OFF[i + 1]], W[i][:, 0:S - Q0[i]], dcy[:, j, 0:S - Q0[i]],
                                            ALU.mult).then_inc(s_mask[j], 1)
                        else:
                            v.tensor_tensor(sf[:, OFF[2]:OFF[3]], W[2][:, 0:256], dcy[:, j, 0:256], ALU.mult)
                            v.tensor_tensor(sf[:, OFF[3] + P:OFF[4]], W[2][:, 256 + P:512], dcy[:, j, 0:P],
                                            ALU.mult).then_inc(s_mask[j], 1)
                    for i, (a, e) in enumerate(((0, 512), (512, 896), (896, 1408))):
                        v.wait_ge(s_sh, n * 3 + i + 1)
                        v.tensor_tensor(sl[:, a:e], sf[:, a:e], sh[:, a:e].bitcast(F32), ALU.subtract).then_inc(s_sl, 1)
                    if not last:
                        queries(n + 1)
                    v.wait_ge(s_of, n + 1 + 1)
                    v.wait_ge(s_gate, n + 1 + 1)
                    v.wait_ge(s_ogl, n + 1)
                    h = nw_of(pair, j)
                    v.scalar_tensor_tensor(out=og[:, :], in0=of[:, :], scalar=h, in1=gate[:, :],
                                           op0=ALU.mult, op1=ALU.mult).then_inc(s_og, 1)
                    v.wait_ge(s_og, n + 1 + 1)
                    v.wait_ge(s_op, n + 1)
                    v.tensor_copy(ogh[:, :], og[:, :]).then_inc(s_ogh, 1)
                    if not last:
                        if j == 1:
                            values(pair + 1)
                        keys(n + 1)

                v.memset(sf[:, OFF[3]:OFF[3] + P], 0.0).then_inc(s_fin, 1)
                v.wait_ge(s_nw, 16)
                with v.Fori(0, B) as b:
                    st = Steps(s_ln, b * LN_STEPS + 1)
                    v.wait_ge(s_x, b * 16 + 16)
                    v.wait_ge(s_xt, b * KD + 1)
                    for t in range(KT):
                        st.did(v.bn_stats(stats[:, t, :], x_in[:, t, :]))
                    st.wait(v)
                    st.did(v.tensor_copy(sm[:, 2, 0:1], stats[:, 0, 0:1]))
                    for t in range(KT):
                        st.did(v.bn_aggr(mv[:, t, :], stats[:, t, :]))
                    st.wait(v)
                    st.did(v.tensor_copy(sm[:, 0, :], mv[:, :, 1]))
                    rsqrt(v, st, sm[:, 1, :], sm[:, 0, :], sm[:, 2, :], sm[:, 3, :], 1.0, LN_EPS)
                    st.wait(v)
                    assert st.n == LN_STEPS
                    for t in range(KT):
                        v.tensor_scalar(normed[:, t, :], x_in[:, t, :], mv[:, t, 0:1], sm[:, 1, t:t + 1],
                                        ALU.subtract, ALU.mult).then_inc(s_normed, 1)
                    for k in range(KD):
                        v.wait_ge(s_xh, b * KD + k + 1)
                        v.tensor_tensor(xTl[:, k, :], W[k][:, :], xTh[:, k, :].bitcast(F32),
                                        ALU.subtract).then_inc(s_xl, 1)
                    queries(b * NH)
                    values(b * NP)
                    keys(b * NH)
                    with v.Fori(0, NP - 1) as p:
                        nw_of = lambda pair, j: nw[:, bass.ds(p * 2 + j, 1)]
                        for j in range(2):
                            slot(b * NP + p, j, False)
                    nw_of = lambda pair, j: nw[:, NH - 2 + j:NH - 1 + j]
                    for j in range(2):
                        slot(b * NP + (NP - 1), j, j == 1)
                    st = Steps(s_fin, b * FIN_STEPS + 1)
                    v.wait_ge(s_ssum, b + 1 + 1)
                    st.did(v.tensor_copy(sm[:, 4, :], W[3][:, :].rearrange("p (t c) -> p t c", c=P)[:, :, 0]))
                    rsqrt(v, st, sm[:, 5, :], sm[:, 4, :], sm[:, 6, :], sm[:, 7, :], float(NH * P), RMS_EPS)
                    st.wait(v)
                    assert st.n == FIN_STEPS
                    v.wait_ge(s_op, b * NH + NH + 1)
                    v.wait_ge(s_xres, b * 16 + 16)
                    v.wait_ge(s_x1out, b * 16 + 1)
                    for t in range(KT):
                        v.scalar_tensor_tensor(out=x1[:, t, :], in0=Y[t][:, :], scalar=sm[:, 5, t:t + 1],
                                               in1=x_res[:, t, :], op0=ALU.mult, op1=ALU.add).then_inc(s_x1, 1)


def tail(nc, c, ctx_rows, ctx_t, pad_mask, x1_dram, out):
    B, S, D = x1_dram.shape
    M = ctx_rows.shape[1]
    F = c.gate_sc.shape[1]
    KD, KT, KF = D // P, S // P, F // P
    FS = spans(F)
    bank, ident, ident16 = c.bank, c.ident, c.ident16
    ctx, sb, sem = scope(nc, "tail")
    with ctx:
        x1, x2, x3 = sb("x1t", [P, D]), sb("x2t", [P, D]), sb("x3t", [P, D])
        h, hT = sb("h", [P, D]), sb("hT", [P, KD, P])
        mem, memT = sb("mem", [M, D]), sb("memT", [P, KD, P])
        mk8 = sb("mk8", [P, B * M // 4], I32)
        mk, mneg = sb("mk", [P, M]), sb("mneg", [P, M])
        stats, mv = sb("stats", [P, 6]), sb("mv", [P, 2])
        sm = sb("sm", [P, 24])
        sc, pr, pT = sb("sc", [P, M]), sb("pr", [P, P]), sb("pT", [M, P])
        xq, mag = sb("xq", [P, D]), sb("mag", [P, F])
        q16, qT = sb("q16", [P, D], F16), sb("qT", [P, KD, P], F16)
        g_, u_, s_ = sb("g_", [P, F]), sb("u_", [P, F]), sb("sg", [P, F])
        t16, tT = sb("t16", [P, F], F16), sb("tT", [P, KF, P], F16)

        s_ld, s_mem, s_out = sem("x1_landed"), sem("memory_landed"), sem("out_stored")
        s_st = sem("tile_steps")
        s_pad, s_mask = sem("pad_cleared"), sem("mask_landed")
        s_h, s_hT, s_hTc = sem("h_ready"), sem("h_turned"), sem("h_turned_copied")
        s_sc, s_max, s_exp = sem("scores_summed2"), sem("max_ready"), sem("exp_ready")
        s_pT, s_pTc, s_rd = sem("p_turned"), sem("p_turned_copied"), sem("readout_summed")
        s_x2 = sem("x2_ready")
        s_q, s_qT, s_qTc = sem("x_quantised"), sem("xq_turned"), sem("xq_turned_copied")
        s_gu = sem("gate_up_summed")
        s_g, s_sig = sem("g_scaled"), sem("g_sigmoid")
        s_t, s_tT, s_tTc = sem("t_quantised"), sem("t_turned"), sem("t_turned_copied")
        s_y, s_fin = sem("down_summed"), sem("out_ready")
        T = B * KT

        prime(nc, [s_rd, s_x2, s_fin, s_tTc, s_out, s_st])
        with nc.Block() as block:
            @block.sync
            def _(sp):
                sp.dma_start(mk8[:, :], pad_mask.rearrange("b m -> () (b m)").to_broadcast([P, B * M // 4])).then_inc(s_mask, 16)
                with sp.Fori(0, B) as b:
                    sp.wait_ge(s_rd, b * KT + 1)
                    sp.wait_ge(s_pad, 2)
                    sp.dma_start(memT[:, :, 0:M], ctx_t[b].rearrange("(k p) m -> p k m", p=P)).then_inc(s_mem, 16)
                    sp.dma_start(mem[:, :], ctx_rows[b]).then_inc(s_mem, 16)
                    with sp.Fori(0, KT) as t:
                        n = b * KT + t
                        sp.wait_ge(s_x2, n + 1)
                        sp.dma_start(x1[:, :], x1_dram[b, bass.ds(t * P, P), :]).then_inc(s_ld, 16)
                        sp.wait_ge(s_fin, n + 1 + 1)
                        sp.dma_start(out[b, bass.ds(t * P, P), :], x3[:, :]).then_inc(s_out, 16)
                sp.wait_ge(s_out, 16 * T + 1)

            @block.gpsimd
            def _(g):
                g.memset(memT[:, :, :], 0.0).then_inc(s_pad, 1)
                g.memset(pr[:, :], 0.0).then_inc(s_pad, 1)

            @block.scalar
            def _(act):
                act.wait_ge(s_pad, 2)
                with act.Fori(0, T) as n:
                    act.wait_ge(s_hT, n + 1)
                    nc.scalar.copy(hT[:, :, :], bank[0][:, :].rearrange("p (k i) -> p k i", i=P)).then_inc(s_hTc, 1)
                    act.wait_ge(s_max, n + 1)
                    nc.scalar.activation(pr[:, 0:M], sc[:, :], ACT.Exp, bias=sm[:, 2:3],
                                         accum_out=sm[:, 3:4]).then_inc(s_exp, 1)
                    act.wait_ge(s_pT, n + 1)
                    nc.scalar.copy(pT[:, :], bank[1][0:M, 0:P]).then_inc(s_pTc, 1)
                    act.wait_ge(s_qT, n + 1)
                    nc.scalar.copy(qT[:, :, :], bank[0][:, 0:KD * P // 2].bitcast(F16)
                                   .rearrange("p (k i) -> p k i", i=P)).then_inc(s_qTc, 1)
                    for i, (a, w) in enumerate(FS):
                        act.wait_ge(s_g, n * 3 + i + 1)
                        nc.scalar.activation(s_[:, a:a + w], g_[:, a:a + w], ACT.Sigmoid).then_inc(s_sig, 1)
                    act.wait_ge(s_tT, n + 1)
                    for i in range(2):
                        k = min(8, KF - 8 * i)
                        nc.scalar.copy(tT[:, 8 * i:8 * i + k, :], bank[i][:, 0:k * P // 2].bitcast(F16)
                                       .rearrange("p (k i) -> p k i", i=P)).then_inc(s_tTc, 1)

            @block.tensor
            def _(pe):
                pe.wait_ge(s_pad, 2)
                with pe.Fori(0, B) as b, pe.Fori(0, KT) as t:
                    n = b * KT + t
                    pe.wait_ge(s_mem, b * 32 + 32)
                    pe.wait_ge(s_h, n + 1)
                    pe.wait_ge(s_tTc, n * 2 + 1)
                    for k in range(KD):
                        mm = pe.transpose(bank[0][:, k * P:(k + 1) * P], h[:, k * P:(k + 1) * P], ident[:, :])
                    mm.then_inc(s_hT, 1)
                    pe.wait_ge(s_hTc, n + 1)
                    for k in range(KD):
                        mm = pe.matmul(bank[1][:, 0:P], hT[:, k, :], memT[:, k, :], start=(k == 0), stop=(k == KD - 1))
                    mm.then_inc(s_sc, 1)
                    pe.wait_ge(s_exp, n + 1)
                    pe.transpose(bank[1][:, 0:P], pr[:, :], ident[:, :]).then_inc(s_pT, 1)
                    pe.wait_ge(s_pTc, n + 1)
                    pe.wait_ge(s_fin, n + 1)
                    pe.matmul(bank[2][:, :], pT[:, :], mem[:, :], start=True, stop=True).then_inc(s_rd, 1)
                    pe.wait_ge(s_q, n + 1)
                    for k in range(KD):
                        mm = pe.transpose(bank[0][:, k * 64:(k + 1) * 64].bitcast(F16), q16[:, k * P:(k + 1) * P],
                                          ident16[:, :])
                    mm.then_inc(s_qT, 1)
                    pe.wait_ge(s_qTc, n + 1)
                    for i, (a, w) in enumerate(FS):
                        for m, wT in enumerate((c.gateT, c.upT)):
                            for k in range(KD):
                                mm = pe.matmul(bank[2 + 2 * i + m][:, 0:w], qT[:, k, :], wT[:, k, a:a + w],
                                               start=(k == 0), stop=(k == KD - 1))
                            mm.then_inc(s_gu, 1)
                    pe.wait_ge(s_t, n + 1)
                    for k in range(KF):
                        mm = pe.transpose(bank[k // 8][:, (k % 8) * 64:(k % 8 + 1) * 64].bitcast(F16),
                                          t16[:, k * P:(k + 1) * P], ident16[:, :])
                    mm.then_inc(s_tT, 1)
                    pe.wait_ge(s_tTc, n * 2 + 2 + 1)
                    for k in range(KF):
                        mm = pe.matmul(bank[2][:, :], tT[:, k, :], c.downT[:, k, :], start=(k == 0), stop=(k == KF - 1))
                    mm.then_inc(s_y, 1)

            @block.vector
            def _(v):
                def norm(st, src):
                    st.wait(v)
                    st.did(v.bn_stats(stats[:, :], src))
                    st.wait(v)
                    st.did(v.tensor_copy(sm[:, 10:11], stats[:, 0:1]))
                    st.did(v.bn_aggr(mv[:, :], stats[:, :]))
                    st.wait(v)
                    rsqrt(v, st, sm[:, 0:1], mv[:, 1:2], sm[:, 10:11], sm[:, 11:12], 1.0, LN_EPS)
                    st.wait(v)

                def row_scale(st, src, named, tmp, s):
                    st.wait(v)
                    st.did(v.tensor_tensor(tmp, src, named, ALU.mult))
                    st.wait(v)
                    st.did(v.tensor_reduce(sm[:, 12:13], tmp, AX, ALU.max, apply_absolute_value=True))
                    st.wait(v)
                    st.did(v.tensor_scalar(sm[:, s:s + 1], sm[:, 12:13], 1.0 / FP8_MAX, None, ALU.mult))
                    st.wait(v)
                    st.did(v.reciprocal(sm[:, s + 1:s + 2], sm[:, s:s + 1]))
                    st.did(v.tensor_scalar(sm[:, s + 2:s + 3], sm[:, s:s + 1], 4.0, None, ALU.mult))
                    st.wait(v)
                    st.did(v.tensor_scalar(tmp, tmp, sm[:, s + 1:s + 2], None, ALU.mult))

                def tile(st, n, first):
                    v.wait_ge(s_ld, n * 16 + 16)
                    norm(st, x1[:, :])
                    v.tensor_scalar(h[:, :], x1[:, :], mv[:, 0:1], sm[:, 0:1], ALU.subtract, ALU.mult).then_inc(s_h, 1)
                    v.wait_ge(s_sc, n + 1)
                    st.did(v.scalar_tensor_tensor(out=sc[:, :], in0=bank[1][:, 0:M], scalar=float(D) ** -0.5,
                                                  in1=mk[:, :], op0=ALU.mult, op1=ALU.mult))
                    st.wait(v)
                    st.did(v.tensor_tensor(sc[:, :], sc[:, :], mneg[:, :], ALU.add))
                    st.wait(v)
                    st.did(v.tensor_reduce(sm[:, 1:2], sc[:, :], AX, ALU.max))
                    st.wait(v)
                    v.tensor_scalar(sm[:, 2:3], sm[:, 1:2], -1.0, None, ALU.mult).then_inc(s_max, 1)
                    v.wait_ge(s_exp, n + 1)
                    st.did(v.reciprocal(sm[:, 4:5], sm[:, 3:4]))
                    st.wait(v)
                    st.did(v.tensor_tensor(sm[:, 5:6], sm[:, 4:5], sm[:, 20:21], ALU.mult))
                    st.wait(v)
                    v.wait_ge(s_rd, n + 1 + 1)
                    v.scalar_tensor_tensor(out=x2[:, :], in0=bank[2][:, :], scalar=sm[:, 5:6], in1=x1[:, :],
                                           op0=ALU.mult, op1=ALU.add).then_inc(s_x2, 1)
                    v.wait_ge(s_x2, n + 1 + 1)
                    norm(st, x2[:, :])
                    st.did(v.tensor_scalar(xq[:, :], x2[:, :], mv[:, 0:1], sm[:, 0:1], ALU.subtract, ALU.mult))
                    row_scale(st, xq[:, :], c.up_named[:, :], xq[:, :], 6)
                    round_fp8(v, st, xq[:, :], mag[:, 0:D], xq[:, :])
                    st.wait(v)
                    v.tensor_copy(q16[:, :], xq[:, :]).then_inc(s_q, 1)
                    for i, (a, w) in enumerate(FS):
                        v.wait_ge(s_gu, n * 6 + 2 * i + 2)
                        v.scalar_tensor_tensor(out=g_[:, a:a + w], in0=bank[2 + 2 * i][:, 0:w], scalar=sm[:, 8:9],
                                               in1=c.gate_sc[:, a:a + w], op0=ALU.mult, op1=ALU.mult).then_inc(s_g, 1)
                        st.did(v.scalar_tensor_tensor(out=u_[:, a:a + w], in0=bank[3 + 2 * i][:, 0:w],
                                                      scalar=sm[:, 8:9], in1=c.up_sc[:, a:a + w],
                                                      op0=ALU.mult, op1=ALU.mult))
                    v.wait_ge(s_g, n * 3 + 3)
                    st.wait(v)
                    st.did(v.tensor_tensor(u_[:, :], u_[:, :], g_[:, :], ALU.mult))
                    v.wait_ge(s_sig, n * 3 + 3)
                    st.wait(v)
                    st.did(v.tensor_tensor(u_[:, :], u_[:, :], s_[:, :], ALU.mult))
                    row_scale(st, u_[:, :], c.down_named[:, :], u_[:, :], 14)
                    round_fp8(v, st, u_[:, :], mag[:, :], u_[:, :])
                    st.wait(v)
                    v.tensor_copy(t16[:, :], u_[:, :]).then_inc(s_t, 1)
                    v.wait_ge(s_y, n + 1)
                    v.wait_ge(s_out, n * 16 + 1)
                    st.did(v.scalar_tensor_tensor(out=x3[:, :], in0=bank[2][:, :], scalar=sm[:, 16:17],
                                                  in1=c.down_sc[:, :], op0=ALU.mult, op1=ALU.mult))
                    st.wait(v)
                    v.tensor_tensor(x3[:, :], x3[:, :], x2[:, :], ALU.add).then_inc(s_fin, 1)

                TILE_STEPS = 2 * 22 + 3 + 2 + 1 + 6 + 4 + 3 + 2 + 6 + 4 + 1
                BATCH_STEPS = 4
                v.wait_ge(s_mask, 16)
                with v.Fori(0, B) as b:
                    base = b * (BATCH_STEPS + KT * TILE_STEPS) + 1
                    st = Steps(s_st, base)
                    st.did(v.tensor_copy(mk[:, :], mk8[:, :].bitcast(U8)[:, bass.ts(b, M)]))
                    st.wait(v)
                    st.did(v.tensor_scalar(mneg[:, :], mk[:, :], -1.0, NEG, ALU.add, ALU.mult))
                    st.did(v.tensor_reduce(sm[:, 20:21], mk[:, :], AX, ALU.max))
                    st.wait(v)
                    st.did(v.tensor_copy(sm[:, 21:22], sm[:, 20:21]))
                    assert st.n == BATCH_STEPS
                    with v.Fori(0, KT) as t:
                        st = Steps(s_st, base + BATCH_STEPS + t * TILE_STEPS)
                        tile(st, b * KT + t, False)
                        assert st.n == TILE_STEPS, st.n


def kernel(x, ctx_2048, mask_BxS2_bk0, L0_attn_slope_rate, L0_attn_w_qkv, L0_attn_w_gate, L0_attn_w_out,
           L0_attn_norm_w, L0_ffn_w_gate, L0_ffn_w_up, L0_ffn_w_down, L0_ffn_up_reorder_index,
           L0_ffn_down_reorder_index):
    import concourse.bacc as bacc
    from concourse.bass_utils import run_bass_kernel_spmd

    x, ctx = np.asarray(x), np.asarray(ctx_2048)
    D = x.shape[2]
    NH = np.asarray(L0_attn_slope_rate).shape[0]
    KD, NP = D // P, NH // 2
    wq = np.asarray(L0_attn_w_qkv).reshape(NP, 2, 3, P, KD, P)
    wq = wq.transpose(0, 5, 4, 1, 2, 3)
    part0 = np.stack([wq[:, :, :, 0, 0], wq[:, :, :, 0, 1], wq[:, :, :, 0, 2], wq[:, :, :, 1, 2]], axis=3)
    part1 = np.stack([wq[:, :, :, 1, 0], wq[:, :, :, 1, 1]], axis=3)
    gates = np.asarray(L0_attn_w_gate).reshape(NP, 2 * P, KD, P).transpose(0, 3, 2, 1)
    outs = np.asarray(L0_attn_w_out).reshape(D, NP, 2, P).transpose(1, 3, 2, 0)
    arrays = {
        "x": x,
        "ctx": ctx,
        "ctx_t": ctx.transpose(0, 2, 1),
        "pad_mask": np.ascontiguousarray(mask_BxS2_bk0).view(np.int32),
        "slope": np.asarray(L0_attn_slope_rate).reshape(1, NH),
        "w_part0": part0.reshape(NP, P, -1),
        "w_part1": part1.reshape(NP, P, -1),
        "w_gates": gates.reshape(NP, P, -1),
        "w_outs": outs.reshape(NP, P, -1),
        "norm_w": np.asarray(L0_attn_norm_w).reshape(NH, P).T,
        "f_gate": np.asarray(L0_ffn_w_gate),
        "f_up": np.asarray(L0_ffn_w_up),
        "f_down": np.asarray(L0_ffn_w_down),
        "up_idx": np.asarray(L0_ffn_up_reorder_index).reshape(-1, P).T,
        "down_idx": np.asarray(L0_ffn_down_reorder_index).reshape(-1, P).T,
    }
    arrays = {f"in_{k}": np.ascontiguousarray(a) for k, a in arrays.items()}
    nc = bacc.Bacc("TRN2", target_bir_lowering=False, num_devices=1)
    args = [nc.dram_tensor(k, a.shape, mybir.dt.from_np(a.dtype), kind="ExternalInput").ap()
            for k, a in arrays.items()]
    out = nc.dram_tensor("out", x.shape, F32, kind="ExternalOutput").ap()
    layer(nc, *args, out)
    r = run_bass_kernel_spmd(nc, [arrays], core_ids=[0])
    return r.results[0]["out"]
```

```python
from contextlib import ExitStack

import numpy as np

import concourse.bass as bass
from concourse import mybir

P = 128
ALU = mybir.AluOpType
ACT = mybir.ActivationFunctionType
AX = mybir.AxisListType.X
F32 = mybir.dt.float32
F32R = mybir.dt.float32r
F16 = mybir.dt.float16
BF16 = mybir.dt.bfloat16
I32 = mybir.dt.int32
U32 = mybir.dt.uint32
U8 = mybir.dt.uint8

LN_EPS = 1e-5
RMS_EPS = 1e-6
NEG = 1e30
EXPONENT_BITS = 0x7F800000
TOP_MANTISSA_BIT = 0x00400000
FP8_MAX = 448.0


class Steps:

    def __init__(self, sem, base=0):
        self.sem, self.base, self.n = sem, base, 0

    def did(self, ins):
        ins.then_inc(self.sem, 1)
        self.n += 1
        return ins

    def wait(self, eng, back=0):
        eng.wait_ge(self.sem, self.base + (self.n - back))


def rsqrt(eng, st, out, x, tmp, tmp2, mean_of, eps):
    st.wait(eng)
    st.did(eng.tensor_scalar(x, x, 1.0 / mean_of, eps, ALU.mult, ALU.add))
    st.wait(eng)
    st.did(eng.tensor_scalar(tmp.bitcast(U32), x.bitcast(U32), 1, None, ALU.logical_shift_right))
    st.wait(eng)
    st.did(eng.tensor_scalar(out.bitcast(I32), tmp.bitcast(I32), -1.0, float(0x5F3759DF), ALU.mult, ALU.add))
    for _ in range(4):
        st.wait(eng)
        st.did(eng.tensor_tensor(tmp, out, out, ALU.mult))
        st.wait(eng)
        st.did(eng.tensor_tensor(tmp2, tmp, x, ALU.mult))
        st.wait(eng)
        st.did(eng.tensor_scalar(tmp, tmp2, -0.5, 1.5, ALU.mult, ALU.add))
        st.wait(eng)
        st.did(eng.tensor_tensor(out, out, tmp, ALU.mult))


SMALL = 2.0 ** -20


def round_e4m3(eng, steps, n, value, small, mag, summed, out, signal):
    eng.tensor_scalar(mag, value.bitcast(U32), EXPONENT_BITS, TOP_MANTISSA_BIT,
                      ALU.bitwise_and, ALU.bitwise_or).then_inc(steps, 1)
    eng.wait_ge(steps, n + 1)
    eng.scalar_tensor_tensor(out=summed, in0=mag.bitcast(F32), scalar=1.5 * 2.0 ** -6, in1=small,
                             op0=ALU.max, op1=ALU.add).then_inc(steps, 1)
    eng.wait_ge(steps, n + 2)
    eng.scalar_tensor_tensor(out=out, in0=mag.bitcast(F32), scalar=1.5 * 2.0 ** -6, in1=summed,
                             op0=ALU.max, op1=ALU.subtract).then_inc(signal, 1)


def layer(nc, x, ctx, ctx_t, pad_mask, slope, w_qkv1, w_qkv2, w_gate, w_out, norm_w, f_gate, f_up, f_down,
          up_idx, down_idx, out):
    B, S, D = x.shape
    NH = slope.shape[1]
    decay_dram = nc.dram_tensor("decay_tables", [NH, P, S], F32, kind="Internal").ap()
    x1_dram = nc.dram_tensor("after_attention", [B, S, D], F32, kind="Internal").ap()
    with ExitStack() as top:
        c = Shared()
        c.ident = top.enter_context(nc.sbuf_tensor("ident", [P, P], F32))
        c.ident_bf = top.enter_context(nc.sbuf_tensor("ident_bf", [P, P], BF16))
        c.ones = top.enter_context(nc.sbuf_tensor("ones", [P, P], F32))
        c.zeros = top.enter_context(nc.sbuf_tensor("zeros", [P, 512], F16))
        c.bank = [top.enter_context(nc.psum_tensor(f"bank{i}", [P, 512], F32)) for i in range(8)]
        constants(nc, c, slope, decay_dram)
        attention(nc, c, x, w_qkv1, w_qkv2, w_gate, w_out, norm_w, decay_dram, x1_dram)
        F = f_gate.shape[0]
        c.gateT = top.enter_context(nc.sbuf_tensor("gateT", [P, D // P, F], F16))
        c.upT = top.enter_context(nc.sbuf_tensor("upT", [P, D // P, F], F16))
        c.downT = top.enter_context(nc.sbuf_tensor("downT", [P, F // P, D], F16))
        c.gate_sc = top.enter_context(nc.sbuf_tensor("gate_sc", [P, F], F32))
        c.up_sc = top.enter_context(nc.sbuf_tensor("up_sc", [P, F], F32))
        c.down_sc = top.enter_context(nc.sbuf_tensor("down_sc", [P, D], F32))
        c.up_named = top.enter_context(nc.sbuf_tensor("up_named", [P, D], F32))
        ffn_weights(nc, c, f_gate, f_up, f_down, up_idx, down_idx)
        tail(nc, c, ctx, ctx_t, pad_mask, x1_dram, out)


class Shared:
    pass


def spans(F):
    return [(a, min(512, F - a)) for a in range(0, F, 512)]


def scope(nc, stage):
    c = ExitStack()
    return (c, lambda name, shape, dt=F32: c.enter_context(nc.sbuf_tensor(f"{stage}_{name}", shape, dt)),
            lambda name: c.enter_context(nc.semaphore(f"{stage}_{name}")))


def prime(nc, semaphores):
    with nc.Block() as block:
        @block.sync
        def _(sp):
            for s in semaphores:
                sp.sem_inc(s, 1)


def constants(nc, c, slope, decay_dram):
    NH, _, S = decay_dram.shape
    ctx, sb, sem = scope(nc, "constants")
    with ctx:
        dist_i = sb("dist_i", [P, S], I32)
        dist = sb("dist", [P, S])
        tri = sb("tri", [P, S])
        slope_b = sb("slope_b", [P, NH])
        dec_e = sb("dec_e", [P, 2, S])
        dec = sb("dec", [P, 2, S])
        s_pool = sem("pool_constants")
        s_in = sem("slope_landed")
        s_dv = sem("dve_constants")
        s_exp = sem("table_exp")
        s_dec = sem("table_ready")
        s_decout = [sem("tables0_stored"), sem("tables1_stored")]
        with nc.Block() as block:
            @block.gpsimd
            def _(g):
                g.memset(c.zeros[:, :], 0.0).then_inc(s_pool, 1)
                g.memset(c.ident[:, :], 0.0).then_inc(s_pool, 1)
                g.memset(c.ones[:, :], 1.0).then_inc(s_pool, 1)
                g.memset(tri[:, :], 1.0).then_inc(s_pool, 1)
                g.iota(dist_i[:, :], [[1, S]], base=0, channel_multiplier=-1).then_inc(s_pool, 1)
                g.wait_ge(s_pool, 5)
                g.affine_select(out=c.ident[:, :], in_=c.ident[:, :], compare_op=ALU.not_equal, fill=1.0,
                                base=0, pattern=[[-1, P]], channel_multiplier=1).then_inc(s_pool, 1)
                g.affine_select(out=tri[:, :], in_=tri[:, :], compare_op=ALU.is_ge, fill=0.0,
                                base=0, pattern=[[1, S]], channel_multiplier=-1).then_inc(s_pool, 1)

            @block.sync
            def _(sp):
                sp.dma_start(slope_b[:, :], slope.to_broadcast([P, NH])).then_inc(s_in, 16)
                for h in range(NH):
                    sp.wait_ge(s_dec, h + 1)
                    sp.dma_start(decay_dram[h], dec[:, h % 2, :]).then_inc(s_decout[h % 2], 16)
                for q in s_decout:
                    sp.wait_ge(q, 16 * NH // 2)

            @block.scalar
            def _(act):
                act.wait_ge(s_dv, 4)
                for h in range(NH):
                    if h >= 2:
                        act.wait_ge(s_dec, h - 1)
                    nc.scalar.activation(dec_e[:, h % 2, :], dist[:, :], ACT.Exp,
                                         scale=slope_b[:, h:h + 1]).then_inc(s_exp, 1)

            @block.vector
            def _(v):
                v.wait_ge(s_pool, 7)
                v.tensor_copy(c.ident_bf[:, :], c.ident[:, :]).then_inc(s_dv, 1)
                v.tensor_copy(dist[:, :], dist_i[:, :]).then_inc(s_dv, 1)
                v.wait_ge(s_dv, 2)
                v.tensor_scalar(dist[:, :], dist[:, :], 0.0, None, ALU.max).then_inc(s_dv, 1)
                v.wait_ge(s_in, 16)
                v.tensor_scalar(slope_b[:, :], slope_b[:, :], -1.0, None, ALU.mult).then_inc(s_dv, 1)
                for h in range(NH):
                    v.wait_ge(s_exp, h + 1)
                    if h >= 2:
                        v.wait_ge(s_decout[h % 2], 16 * (h // 2))
                    v.tensor_tensor(dec[:, h % 2, :], dec_e[:, h % 2, :], tri[:, :], ALU.mult).then_inc(s_dec, 1)


def ffn_weights(nc, c, f_gate, f_up, f_down, up_idx, down_idx):
    F, D = f_gate.shape
    KD, KF = D // P, F // P
    FS = spans(F)
    ident, bank = c.ident, c.bank
    tasks = [(k, t) for t in range(KF) for k in "gu"] + [("d", t) for t in range(KD)]
    width = [F if k == "d" else D for k, _ in tasks]
    NT = len(tasks)
    ctx, sb, sem = scope(nc, "ffn_weights")
    with ctx:
        col_i, col = sb("col_i", [P, F], I32), sb("col", [P, F])
        uix, dix = sb("uix", [P, KD], I32), sb("dix", [P, KF], I32)
        uixf, dixf = sb("uixf", [P, KD]), sb("dixf", [P, KF])
        hot, ones16 = sb("hot", [P, 2, F], F16), sb("ones16", [P, P], F16)
        up_cnt, down_cnt = sb("up_cnt", [P, D]), sb("down_cnt", [P, F])
        down_named = sb("down_named", [P, F])
        cnt_col = sb("cnt_col", [P, KD + KF])
        rows, w_v = sb("rows", [P, 2, F]), sb("w_v", [P, 2, F])
        v32, v_small = sb("v32", [P, 2, F]), sb("v_small", [P, 2, F])
        mag, summed = sb("mag", [P, F], U32), sb("summed", [P, F])
        w_q = sb("w_q", [P, 2, F], BF16)
        w_s = sb("w_s", [P, 2, 4])
        diag = sb("diag", [P, 2, P])
        s_pool, s_ix, s_dv = sem("pool_iota"), sem("indices_landed"), sem("count_steps")
        s_hot, s_cnt = sem("one_hot_ready"), sem("counts_summed")
        s_turn, s_col = sem("counts_turned"), sem("counts_ready")
        s_rows = [sem("rows0_landed"), sem("rows1_landed")]
        s_named, s_small = sem("rows_masked"), sem("row_scale_steps")
        s_v, s_vs = sem("scaled_ready"), sem("scaled_small_ready")
        s_round, s_quant, s_diag = sem("rounding_steps"), sem("rows_quantised"), sem("scale_diagonal")
        s_tr, s_spread = sem("rows_turned"), sem("scales_spread")
        s_evac, s_scale = sem("turned_copied"), sem("scales_copied")
        with nc.Block() as block:
            @block.gpsimd
            def _(g):
                def load(n):
                    kind, t = tasks[n]
                    if kind == "d":
                        g.dma_start(rows[:, n % 2, :], f_down[t * P:(t + 1) * P, :]).then_inc(s_rows[n % 2], 16)
                    else:
                        g.indirect_dma_start(rows[:, n % 2, 0:D], None, f_gate if kind == "g" else f_up,
                                             bass.IndirectOffsetOnAxis(ap=dix[:, t:t + 1], axis=0)
                                             ).then_inc(s_rows[n % 2], 16)

                g.memset(ones16[:, :], 1.0).then_inc(s_pool, 1)
                g.iota(col_i[:, :], [[1, F]], base=0, channel_multiplier=0).then_inc(s_pool, 1)
                g.wait_ge(s_ix, 32)
                load(0)
                load(1)
                g.wait_ge(s_col, KD + KF)
                for n, (kind, t) in enumerate(tasks):
                    w = width[n]
                    g.wait_ge(s_rows[n % 2], 16 * (n // 2 + 1))
                    if n >= 2:
                        g.wait_ge(s_vs, n - 1)
                    g.tensor_tensor(w_v[:, n % 2, 0:w], rows[:, n % 2, 0:w],
                                    (down_named if kind == "d" else c.up_named)[:, 0:w], ALU.mult).then_inc(s_named, 1)
                    if n + 2 < NT:
                        g.wait_ge(s_named, n + 1)
                        load(n + 2)

            @block.sync
            def _(sp):
                sp.dma_start(uix[:, :], up_idx).then_inc(s_ix, 16)
                sp.dma_start(dix[:, :], down_idx).then_inc(s_ix, 16)

            @block.scalar
            def _(act):
                def scaled(n):
                    w, s = width[n], n % 2
                    act.wait_ge(s_small, 4 * n + 4)
                    if n >= 2:
                        act.wait_ge(s_quant, n - 1)
                    nc.scalar.activation(v32[:, s, 0:w], w_v[:, s, 0:w], ACT.Copy,
                                         scale=w_s[:, s, 2:3]).then_inc(s_v, 1)
                    nc.scalar.activation(v_small[:, s, 0:w], w_v[:, s, 0:w], ACT.Copy,
                                         scale=w_s[:, s, 3:4]).then_inc(s_vs, 1)

                scaled(0)
                for n, (kind, t) in enumerate(tasks):
                    if n + 1 < NT:
                        scaled(n + 1)
                    dst = {"g": c.gateT, "u": c.upT, "d": c.downT}[kind]
                    first, nb = (KD, KF) if kind == "d" else (0, KD)
                    act.wait_ge(s_tr, n + 1)
                    for k in range(nb):
                        ins = nc.scalar.activation(
                            dst[:, k, t * P:(t + 1) * P],
                            bank[2 * (n % 2) + k // 8][:, (k % 8) * 64:(k % 8 + 1) * 64].bitcast(BF16),
                            ACT.Copy, scale=cnt_col[:, first + k:first + k + 1])
                    ins.then_inc(s_evac, 1)

            @block.tensor
            def _(pe):
                pe.wait_ge(s_pool, 2)
                for n in range(KD):
                    pe.wait_ge(s_hot, n + 1)
                    pe.matmul(bank[3][:, 0:D], ones16[:, :], hot[:, n % 2, 0:D], start=(n == 0),
                              stop=(n == KD - 1)).then_inc(s_cnt, 1)
                for n in range(KF):
                    pe.wait_ge(s_hot, KD + n + 1)
                    for i, (a, w) in enumerate(FS):
                        mm = pe.matmul(bank[4 + i][:, 0:w], ones16[:, :], hot[:, (KD + n) % 2, a:a + w],
                                       start=(n == 0), stop=(n == KF - 1))
                    mm.then_inc(s_cnt, 1)
                for n in range(KD + KF):
                    pe.wait_ge(s_dv, 3 + 2 * (1 + len(FS)))
                    if n >= 2:
                        pe.wait_ge(s_col, n - 1)
                    src = up_cnt[:, n * P:(n + 1) * P] if n < KD else down_cnt[:, (n - KD) * P:(n - KD + 1) * P]
                    pe.transpose(bank[n % 2][:, 0:P], src, ident[:, :]).then_inc(s_turn, 1)
                for n, (kind, t) in enumerate(tasks):
                    pe.wait_ge(s_quant, n + 1)
                    pe.wait_ge(s_col, KD + KF)
                    if n >= 2:
                        pe.wait_ge(s_evac, n - 1)
                    for k in range(KF if kind == "d" else KD):
                        mm = pe.transpose(bank[2 * (n % 2) + k // 8][:, (k % 8) * 64:(k % 8 + 1) * 64].bitcast(BF16),
                                          w_q[:, n % 2, k * P:(k + 1) * P], c.ident_bf[:, :])
                    mm.then_inc(s_tr, 1)
                    pe.wait_ge(s_diag, n + 1)
                    if n >= 2:
                        pe.wait_ge(s_scale, n - 1)
                    pe.matmul(bank[6 + n % 2][:, 0:P], c.ones[:, :], diag[:, n % 2, :], start=True,
                              stop=True).then_inc(s_spread, 1)

            @block.vector
            def _(v):
                def row_scale(n):
                    w, s = width[n], n % 2
                    v.wait_ge(s_named, n + 1)
                    if n >= 2:
                        v.wait_ge(s_vs, n - 1)
                        v.wait_ge(s_diag, n - 1)
                    v.tensor_reduce(w_s[:, s, 0:1], w_v[:, s, 0:w], AX, ALU.max,
                                    apply_absolute_value=True).then_inc(s_small, 1)
                    v.wait_ge(s_small, 4 * n + 1)
                    v.tensor_scalar(w_s[:, s, 1:2], w_s[:, s, 0:1], 1.0 / FP8_MAX, None, ALU.mult).then_inc(s_small, 1)
                    v.wait_ge(s_small, 4 * n + 2)
                    v.reciprocal(w_s[:, s, 2:3], w_s[:, s, 1:2]).then_inc(s_small, 1)
                    v.wait_ge(s_small, 4 * n + 3)
                    v.tensor_scalar(w_s[:, s, 3:4], w_s[:, s, 2:3], SMALL, None, ALU.mult).then_inc(s_small, 1)

                def spread(n):
                    kind, t = tasks[n]
                    v.wait_ge(s_spread, n + 1)
                    dst = {"g": c.gate_sc, "u": c.up_sc, "d": c.down_sc}[kind][:, t * P:(t + 1) * P]
                    if kind == "u":
                        v.tensor_tensor(dst, bank[6 + n % 2][:, 0:P], down_named[:, t * P:(t + 1) * P],
                                        ALU.mult).then_inc(s_scale, 1)
                    else:
                        v.tensor_copy(dst, bank[6 + n % 2][:, 0:P]).then_inc(s_scale, 1)

                st = Steps(s_dv)
                v.wait_ge(s_pool, 2)
                st.did(v.tensor_copy(col[:, :], col_i[:, :]))
                v.wait_ge(s_ix, 32)
                st.did(v.tensor_copy(uixf[:, :], uix[:, :]))
                st.did(v.tensor_copy(dixf[:, :], dix[:, :]))
                st.wait(v)
                for n in range(KD + KF):
                    if n >= 2:
                        v.wait_ge(s_cnt, n - 1)
                    w, ix = (D, uixf[:, n:n + 1]) if n < KD else (F, dixf[:, n - KD:n - KD + 1])
                    v.tensor_scalar(hot[:, n % 2, 0:w], col[:, 0:w], ix, None, ALU.is_equal).then_inc(s_hot, 1)
                v.wait_ge(s_cnt, KD + KF)
                for named, cnt, parts in ((c.up_named, up_cnt, [(3, 0, D)]),
                                          (down_named, down_cnt, [(4 + i, a, w) for i, (a, w) in enumerate(FS)])):
                    for b, a, w in parts:
                        st.did(v.tensor_scalar(named[:, a:a + w], bank[b][:, 0:w], 1.0, None, ALU.min))
                        st.did(v.tensor_scalar(cnt[:, a:a + w], bank[b][:, 0:w], -(2.0 ** 18), None, ALU.mult))
                for n in range(KD + KF):
                    v.wait_ge(s_turn, n + 1)
                    v.tensor_copy(cnt_col[:, n:n + 1], bank[n % 2][:, 0:1]).then_inc(s_col, 1)
                row_scale(0)
                for n in range(NT):
                    if n + 1 < NT:
                        row_scale(n + 1)
                    w, s = width[n], n % 2
                    if n >= 2:
                        v.wait_ge(s_spread, n - 1)
                    v.tensor_scalar(diag[:, s, :], ident[:, :], w_s[:, s, 1:2], None, ALU.mult).then_inc(s_diag, 1)
                    v.wait_ge(s_v, n + 1)
                    v.wait_ge(s_vs, n + 1)
                    if n >= 2:
                        v.wait_ge(s_tr, n - 1)
                    if n:
                        v.wait_ge(s_quant, n)
                    round_e4m3(v, s_round, 2 * n, v32[:, s, 0:w], v_small[:, s, 0:w], mag[:, 0:w], summed[:, 0:w],
                               w_q[:, s, 0:w], s_quant)
                    if n:
                        spread(n - 1)
                spread(NT - 1)


def attention(nc, c, x, w_qkv1, w_qkv2, w_gate, w_out, norm_w, decay_dram, x1_dram):
    B, S, D = x.shape
    NH = decay_dram.shape[0]
    KD, KT, NP = D // P, S // P, NH // 2
    assert KD == 4 and KT == 4
    ident, bank = c.ident, c.bank
    ctx, sb, sem = scope(nc, "attention")
    with ctx:
        x_in, normed = sb("x_in", [P, KT, D]), sb("normed", [P, KT, D])
        x_res, x1 = sb("x_res", [P, KT, D]), sb("x1", [P, KT, D])
        stats, mv = sb("stats", [P, KT, 6]), sb("mv", [P, KT, 2])
        sm = sb("sm", [P, 8, KT])
        xTh, xTl = sb("xTh", [P, KD, S], F32R), sb("xTl", [P, KD, S], F32R)
        WN = [KD * 4 * P, KD * 2 * P, KD * 2 * P, 2 * D]
        raw = [sb(f"raw{i}", [P, n]) for i, n in enumerate(WN)]
        wh = [sb(f"w_hi{i}", [P, n], F32R) for i, n in enumerate(WN)]
        wl = [sb(f"w_lo{i}", [P, n], F32R) for i, n in enumerate(WN)]
        w_src = [w_qkv1, w_qkv2, w_gate, w_out]
        nw = sb("nw", [P, NH])
        dcy = sb("dcy", [P, 2, S])
        sig_q, sig_k, sig_v = sb("sig_q", [P, S]), sb("sig_k", [P, S]), sb("sig_v", [P, KT, 2 * P])
        qf, kf, vf = sb("qf", [P, S]), sb("kf", [P, S]), sb("vf", [P, KT, 2 * P])
        qh, ql = sb("qh", [P, S], F32R), sb("ql", [P, S], F32R)
        kh, kl = sb("kh", [P, S], F32R), sb("kl", [P, S], F32R)
        vh, vl = sb("vh", [P, KT, 2 * P], F32R), sb("vl", [P, KT, 2 * P], F32R)
        Q0 = [0, 128, 256, 256]
        OFF = [0, 512, 896, 1152, 1408]
        sf = sb("sf", [P, OFF[4]])
        sh, sl = sb("sh", [P, OFF[4]], F32R), sb("sl", [P, OFF[4]], F32R)
        gate, of, og = sb("gate", [P, S]), sb("of", [P, S]), sb("og", [P, S])
        ogh, ogl = sb("ogh", [P, S], F32R), sb("ogl", [P, S], F32R)
        sq, sq_sum = sb("sq", [P, S]), sb("sq_sum", [P, S])
        W, Y = bank[0:4], bank[4:8]
        part = [[t.rearrange("p (k c) -> p k c", k=k) for t, k in zip(ws, (KD, KD, KD, 2))] for ws in
                ([w[:, :] for w in wh], [w[:, :] for w in wl])]

        s_x, s_xres, s_nw = sem("x_landed"), sem("x_res_landed"), sem("norm_w_landed")
        s_raw = [sem(f"raw{i}_landed") for i in range(4)]
        s_wh = [sem(f"w{i}_hi_ready") for i in range(4)]
        s_wl = [sem(f"w{i}_lo_ready") for i in range(4)]
        s_dcy = [sem(f"decay{i}_landed") for i in range(2)]
        s_ln, s_normed, s_xt = sem("norm_steps"), sem("normed_ready"), sem("x_turned")
        s_xh, s_xl = sem("x_hi_ready"), sem("x_lo_ready")
        s_q, s_k, s_v = sem("q_summed"), sem("k_summed"), sem("v_summed")
        s_s, s_g, s_o, s_op = sem("scores_summed"), sem("gate_summed"), sem("o_summed"), sem("y_added")
        s_sigq, s_sigk, s_sigv = sem("q_sigmoid"), sem("k_sigmoid"), sem("v_sigmoid")
        s_qm, s_km, s_vm = sem("q_ready"), sem("k_ready"), sem("v_ready")
        s_qh, s_kh, s_vh = sem("q_hi_ready"), sem("k_hi_ready"), sem("v_hi_ready")
        s_ql, s_kl, s_vl = sem("q_lo_ready"), sem("k_lo_ready"), sem("v_lo_ready")
        s_mask = [sem("scores_decayed0"), sem("scores_decayed1")]
        s_sh, s_sl = sem("scores_hi_ready"), sem("scores_lo_ready")
        s_gate, s_of, s_og = sem("gate_ready"), sem("o_copied"), sem("gated")
        s_ogh, s_ogl = sem("gated_hi_ready"), sem("gated_lo_ready")
        s_sq, s_acc, s_zero = sem("o_squared"), sem("squares_added"), sem("squares_cleared")
        s_ssum, s_fin = sem("squares_summed"), sem("batch_end_steps")
        s_x1, s_x1out = sem("x1_ready"), sem("x1_stored")
        LN_STEPS, FIN_STEPS = 2 * KT + 2 + 19, 1 + 19

        prime(nc, [s_normed, *s_wh, *s_wl, *s_mask, s_x1, s_ssum, s_op, s_acc, s_qm, s_km, s_vm, s_o, s_og, s_sq, s_of,
                   s_gate, s_ogl, s_x1out, s_xt, s_ln])
        PASSES = [(0, 0), (0, 1), (1, 0)]

        with nc.Block() as block:
            @block.sync
            def _(sp):
                def load(i, p, n):
                    sp.wait_ge(s_wh[i], n + 1)
                    sp.wait_ge(s_wl[i], n + 1)
                    sp.dma_start(raw[i][:, :], w_src[i][p]).then_inc(s_raw[i], 16)

                sp.dma_start(nw[:, :], norm_w).then_inc(s_nw, 16)
                with sp.Fori(0, B) as b:
                    sp.wait_ge(s_normed, KT * b + 1)
                    sp.dma_start(x_in[:, :, :], x[b].rearrange("(t p) d -> p t d", p=P)).then_inc(s_x, 16)
                    with sp.Fori(0, NP) as p:
                        n = b * NP + p
                        for i in range(4):
                            load(i, p, n)
                        for j in range(2):
                            sp.wait_ge(s_mask[j], n * 3 + 1)
                            sp.dma_start(dcy[:, j, :], decay_dram[p * 2 + j]).then_inc(s_dcy[j], 16)
                for i in range(3):
                    load(i, 0, B * NP)

            @block.gpsimd
            def _(g):
                def weights_lo(i, n):
                    g.wait_ge(s_wh[i], n + 1 + 1)
                    g.tensor_tensor(wl[i][:, :], raw[i][:, :], wh[i][:, :].bitcast(F32), ALU.subtract).then_inc(s_wl[i], 1)

                def slot(pair, j, b):
                    n = pair * 2 + j
                    if j == 0:
                        weights_lo(3, pair)
                    g.wait_ge(s_acc, n + 1)
                    g.wait_ge(s_of, n + 1 + 1)
                    g.tensor_tensor(sq[:, :], of[:, :], of[:, :], ALU.mult).then_inc(s_sq, 1)
                    g.wait_ge(s_ogh, n + 1)
                    g.wait_ge(s_op, n + 1)
                    g.tensor_tensor(ogl[:, :], og[:, :], ogh[:, :].bitcast(F32), ALU.subtract).then_inc(s_ogl, 1)
                    g.wait_ge(s_sq, n + 1 + 1)
                    g.wait_ge(s_acc, n + 1)
                    g.wait_ge(s_zero, b + 1)
                    g.tensor_tensor(sq_sum[:, :], sq_sum[:, :], sq[:, :], ALU.add).then_inc(s_acc, 1)
                    for i in ((0,) if j == 0 else (2, 1)):
                        weights_lo(i, pair + 1)

                for i in range(3):
                    weights_lo(i, 0)
                with g.Fori(0, B) as b:
                    g.wait_ge(s_x1, KT * b + 1)
                    g.dma_start(x_res[:, :, :], x[b].rearrange("(t p) d -> p t d", p=P)).then_inc(s_xres, 16)
                    g.wait_ge(s_ssum, b + 1)
                    g.tensor_tensor(sq_sum[:, :], c.zeros[:, :], c.zeros[:, :], ALU.add).then_inc(s_zero, 1)
                    with g.Fori(0, NP) as p:
                        for j in range(2):
                            slot(b * NP + p, j, b)

            @block.scalar
            def _(act):
                def weights_hi(i, n):
                    act.wait_ge(s_raw[i], 16 * n + 16)
                    nc.scalar.copy(wh[i][:, :], raw[i][:, :]).then_inc(s_wh[i], 1)

                def sig(dst, src, ready, n, used, signal):
                    act.wait_ge(ready, n + 1)
                    act.wait_ge(used, n + 1)
                    nc.scalar.activation(dst, src, ACT.Sigmoid).then_inc(signal, 1)

                def sig_values(pair):
                    for i in range(2):
                        act.wait_ge(s_v, pair * 2 + i + 1)
                        act.wait_ge(s_vm, pair * 2 + 1)
                        nc.scalar.activation(sig_v[:, 2 * i:2 * i + 2, :],
                                             W[2 + i][:, :].rearrange("p (t c) -> p t c", t=2),
                                             ACT.Sigmoid).then_inc(s_sigv, 1)

                def slot(pair, j, last):
                    n = pair * 2 + j
                    for i, (a, e) in enumerate(((0, 512), (512, 896), (896, 1408))):
                        act.wait_ge(s_mask[j], pair * 3 + i + 1 + 1)
                        act.wait_ge(s_o, n + 1)
                        nc.scalar.copy(sh[:, a:e], sf[:, a:e]).then_inc(s_sh, 1)
                    sig(gate[:, :], W[3][:, :], s_g, n, s_og, s_gate)
                    if j == 0:
                        act.wait_ge(s_op, n + 1)
                        weights_hi(3, pair)
                    if not last:
                        sig(sig_q[:, :], W[0][:, :], s_q, n + 1, s_qm, s_sigq)
                    if j == 1:
                        act.wait_ge(s_g, n + 1)
                        weights_hi(2, pair + 1)
                    act.wait_ge(s_o, n + 1 + 1)
                    act.wait_ge(s_og, n + 1)
                    act.wait_ge(s_sq, n + 1)
                    nc.scalar.copy(of[:, :], W[1][:, :]).then_inc(s_of, 1)
                    if not last:
                        if j == 1:
                            sig_values(pair + 1)
                        sig(sig_k[:, :], W[0][:, :], s_k, n + 1, s_km, s_sigk)
                    if j == 0:
                        act.wait_ge(s_k, n + 1)
                        weights_hi(0, pair + 1)
                    else:
                        act.wait_ge(s_k, n + 1)
                        weights_hi(1, pair + 1)

                for i in range(3):
                    weights_hi(i, 0)
                with act.Fori(0, B) as b:
                    for k in range(KD):
                        act.wait_ge(s_xt, KD * b + k + 1 + 1)
                        nc.scalar.copy(xTh[:, k, :], W[k][:, :]).then_inc(s_xh, 1)
                    sig(sig_q[:, :], W[0][:, :], s_q, b * NH, s_qm, s_sigq)
                    sig_values(b * NP)
                    sig(sig_k[:, :], W[0][:, :], s_k, b * NH, s_km, s_sigk)
                    with act.Fori(0, NP - 1) as p:
                        for j in range(2):
                            slot(b * NP + p, j, False)
                    for j in range(2):
                        slot(b * NP + (NP - 1), j, j == 1)
                    act.wait_ge(s_x1, KT * b + KT + 1)
                    act.dma_start(x1_dram[b].rearrange("(t p) d -> p t d", p=P), x1[:, :, :]).then_inc(s_x1out, 16)
                act.wait_ge(s_x1out, 16 * B + 1)

            @block.tensor
            def _(pe):
                def head_rows(dst, i, col):
                    for k in range(KD):
                        for n, (a, b) in enumerate(PASSES):
                            mm = pe.matmul(dst, part[a][i][:, k, col:col + P], (xTh, xTl)[b][:, k, :],
                                           start=(k == 0 and n == 0), stop=(k == KD - 1 and n == 2))
                    return mm

                def wait_part(i, n):
                    pe.wait_ge(s_wh[i], n + 1 + 1)
                    pe.wait_ge(s_wl[i], n + 1 + 1)

                def values(pair):
                    for t in range(KT):
                        for k in range(KD):
                            for n, (a, b) in enumerate(PASSES):
                                mm = pe.matmul(W[2 + t // 2][:, (t % 2) * 2 * P:(t % 2 + 1) * 2 * P],
                                               (xTh, xTl)[b][:, k, t * P:(t + 1) * P],
                                               part[a][0][:, k, 2 * P:4 * P],
                                               start=(k == 0 and n == 0), stop=(k == KD - 1 and n == 2))
                        if t % 2:
                            mm.then_inc(s_v, 1)

                def slot(pair, j, last):
                    n = pair * 2 + j
                    pe.wait_ge(s_qh, n + 1)
                    pe.wait_ge(s_ql, n + 1)
                    pe.wait_ge(s_kh, n + 1)
                    pe.wait_ge(s_kl, n + 1)
                    for t in range(KT):
                        dst = W[min(t, 2)][:, (256 if t == 3 else 0):(256 if t == 3 else 0) + S - Q0[t]]
                        if t == 1:
                            pe.wait_ge(s_of, n + 1)
                        if t == 2:
                            pe.wait_ge(s_vm, pair * 2 + 2 + 1)
                        for i, (a, b) in enumerate(PASSES):
                            mm = pe.matmul(dst, (kh, kl)[a][:, t * P:(t + 1) * P], (qh, ql)[b][:, Q0[t]:S],
                                           start=(i == 0), stop=(i == 2))
                        if t != 2:
                            mm.then_inc(s_s, 1)
                    wait_part(2, pair)
                    head_rows(W[3][:, :], 2, j * P).then_inc(s_g, 1)
                    if not last:
                        wait_part(1 if j == 0 else 0, pair + j)
                        pe.wait_ge(s_mask[j], pair * 3 + 1 + 1)
                        head_rows(W[0][:, :], 1 if j == 0 else 0, 0).then_inc(s_q, 1)
                    pe.wait_ge(s_vh, pair + 1)
                    pe.wait_ge(s_vl, pair + 1)
                    pe.wait_ge(s_sh, n * 3 + 3)
                    pe.wait_ge(s_sl, n * 3 + 3)
                    for t in range(KT):
                        for i, (a, b) in enumerate(PASSES):
                            mm = pe.matmul(W[1][:, Q0[t]:S], (vh, vl)[a][:, t, j * P:(j + 1) * P],
                                           (sh, sl)[b][:, OFF[t]:OFF[t + 1]],
                                           start=(t == 0 and i == 0), stop=(t == KT - 1 and i == 2),
                                           skip_group_check=True)
                    mm.then_inc(s_o, 1)
                    if not last:
                        if j == 1:
                            pe.wait_ge(s_gate, n + 1 + 1)
                            values(pair + 1)
                        pe.wait_ge(s_qm, n + 2 + 1)
                        head_rows(W[0][:, :], 1 if j == 0 else 0, P).then_inc(s_k, 1)
                    pe.wait_ge(s_ogh, n + 1)
                    pe.wait_ge(s_ogl, n + 1 + 1)
                    wait_part(3, pair)
                    for t in range(KT):
                        for i, (a, b) in enumerate(PASSES):
                            mm = pe.matmul(Y[t][:, :], (ogh, ogl)[a][:, t * P:(t + 1) * P], part[b][3][:, j, :],
                                           start=False, stop=False, skip_group_check=True)
                    mm.then_inc(s_op, 1)

                with pe.Fori(0, B) as b:
                    pe.wait_ge(s_normed, KT * b + KT + 1)
                    pe.wait_ge(s_of, NH * b + 1)
                    pe.wait_ge(s_gate, NH * b + 1)
                    for k in range(KD):
                        for t in range(KT):
                            mm = pe.transpose(W[k][:, t * P:(t + 1) * P], normed[:, t, k * P:(k + 1) * P], ident[:, :])
                        mm.then_inc(s_xt, 1)
                    for t in range(KT):
                        pe.matmul(Y[t][:, :], c.zeros[:, 0:P], c.zeros[:, :], start=True, stop=False,
                                  skip_group_check=True)
                    pe.wait_ge(s_xh, KD * b + KD)
                    pe.wait_ge(s_xl, KD * b + KD)
                    wait_part(0, b * NP)
                    head_rows(W[0][:, :], 0, 0).then_inc(s_q, 1)
                    values(b * NP)
                    pe.wait_ge(s_qm, b * NH + 1 + 1)
                    head_rows(W[0][:, :], 0, P).then_inc(s_k, 1)
                    with pe.Fori(0, NP - 1) as p:
                        for j in range(2):
                            slot(b * NP + p, j, False)
                    for j in range(2):
                        slot(b * NP + (NP - 1), j, j == 1)
                    pe.wait_ge(s_acc, b * NH + NH + 1)
                    pe.wait_ge(s_gate, b * NH + NH + 1)
                    for t in range(KT):
                        mm = pe.matmul(W[3][:, t * P:(t + 1) * P], sq_sum[:, t * P:(t + 1) * P], c.ones[:, :],
                                       start=True, stop=True)
                    mm.then_inc(s_ssum, 1)

            @block.vector
            def _(v):
                def split(f, h, l, ready, n, hi, lo):
                    v.wait_ge(ready, n)
                    v.tensor_copy(h, f).then_inc(hi, 1)

                def silu_split(n, src, sg, f, h, l, sigd, made, hi, lo):
                    v.wait_ge(sigd, n + 1)
                    v.tensor_tensor(f[:, :], src, sg[:, :], ALU.mult).then_inc(made, 1)
                    v.wait_ge(made, n + 2)
                    v.tensor_copy(h[:, :], f[:, :]).then_inc(hi, 1)
                    v.wait_ge(hi, n + 1)
                    v.tensor_tensor(l[:, :], f[:, :], h[:, :].bitcast(F32), ALU.subtract).then_inc(lo, 1)

                def queries(n):
                    silu_split(n, W[0][:, :], sig_q, qf, qh, ql, s_sigq, s_qm, s_qh, s_ql)

                def keys(n):
                    silu_split(n, W[0][:, :], sig_k, kf, kh, kl, s_sigk, s_km, s_kh, s_kl)

                def values(pair):
                    for i in range(2):
                        v.wait_ge(s_sigv, pair * 2 + i + 1)
                        v.tensor_tensor(vf[:, 2 * i:2 * i + 2, :], W[2 + i][:, :].rearrange("p (t c) -> p t c", t=2),
                                        sig_v[:, 2 * i:2 * i + 2, :], ALU.mult).then_inc(s_vm, 1)
                    v.wait_ge(s_vm, pair * 2 + 2 + 1)
                    v.tensor_copy(vh[:, :, :], vf[:, :, :]).then_inc(s_vh, 1)
                    v.wait_ge(s_vh, pair + 1)
                    v.tensor_tensor(vl[:, :, :], vf[:, :, :], vh[:, :, :].bitcast(F32), ALU.subtract).then_inc(s_vl, 1)

                def slot(pair, j, last):
                    n = pair * 2 + j
                    v.wait_ge(s_dcy[j], pair * 16 + 16)
                    for i in range(3):
                        v.wait_ge(s_s, n * 3 + i + 1)
                        if i < 2:
                            v.tensor_tensor(sf[:, OFF[i]:OFF[i + 1]], W[i][:, 0:S - Q0[i]], dcy[:, j, 0:S - Q0[i]],
                                            ALU.mult).then_inc(s_mask[j], 1)
                        else:
                            v.tensor_tensor(sf[:, OFF[2]:OFF[3]], W[2][:, 0:256], dcy[:, j, 0:256], ALU.mult)
                            v.tensor_tensor(sf[:, OFF[3] + P:OFF[4]], W[2][:, 256 + P:512], dcy[:, j, 0:P],
                                            ALU.mult).then_inc(s_mask[j], 1)
                    for i, (a, e) in enumerate(((0, 512), (512, 896), (896, 1408))):
                        v.wait_ge(s_sh, n * 3 + i + 1)
                        v.tensor_tensor(sl[:, a:e], sf[:, a:e], sh[:, a:e].bitcast(F32), ALU.subtract).then_inc(s_sl, 1)
                    if not last:
                        queries(n + 1)
                    v.wait_ge(s_of, n + 1 + 1)
                    v.wait_ge(s_gate, n + 1 + 1)
                    v.wait_ge(s_ogl, n + 1)
                    h = nw_of(pair, j)
                    v.scalar_tensor_tensor(out=og[:, :], in0=of[:, :], scalar=h, in1=gate[:, :],
                                           op0=ALU.mult, op1=ALU.mult).then_inc(s_og, 1)
                    v.wait_ge(s_og, n + 1 + 1)
                    v.wait_ge(s_op, n + 1)
                    v.tensor_copy(ogh[:, :], og[:, :]).then_inc(s_ogh, 1)
                    if not last:
                        if j == 1:
                            values(pair + 1)
                        keys(n + 1)

                v.memset(sf[:, OFF[3]:OFF[3] + P], 0.0).then_inc(s_fin, 1)
                v.wait_ge(s_nw, 16)
                with v.Fori(0, B) as b:
                    st = Steps(s_ln, b * LN_STEPS + 1)
                    v.wait_ge(s_x, b * 16 + 16)
                    v.wait_ge(s_xt, b * KD + 1)
                    for t in range(KT):
                        st.did(v.bn_stats(stats[:, t, :], x_in[:, t, :]))
                    st.wait(v)
                    st.did(v.tensor_copy(sm[:, 2, 0:1], stats[:, 0, 0:1]))
                    for t in range(KT):
                        st.did(v.bn_aggr(mv[:, t, :], stats[:, t, :]))
                    st.wait(v)
                    st.did(v.tensor_copy(sm[:, 0, :], mv[:, :, 1]))
                    rsqrt(v, st, sm[:, 1, :], sm[:, 0, :], sm[:, 2, :], sm[:, 3, :], 1.0, LN_EPS)
                    st.wait(v)
                    assert st.n == LN_STEPS
                    for t in range(KT):
                        v.tensor_scalar(normed[:, t, :], x_in[:, t, :], mv[:, t, 0:1], sm[:, 1, t:t + 1],
                                        ALU.subtract, ALU.mult).then_inc(s_normed, 1)
                    for k in range(KD):
                        v.wait_ge(s_xh, b * KD + k + 1)
                        v.tensor_tensor(xTl[:, k, :], W[k][:, :], xTh[:, k, :].bitcast(F32),
                                        ALU.subtract).then_inc(s_xl, 1)
                    queries(b * NH)
                    values(b * NP)
                    keys(b * NH)
                    with v.Fori(0, NP - 1) as p:
                        nw_of = lambda pair, j: nw[:, bass.ds(p * 2 + j, 1)]
                        for j in range(2):
                            slot(b * NP + p, j, False)
                    nw_of = lambda pair, j: nw[:, NH - 2 + j:NH - 1 + j]
                    for j in range(2):
                        slot(b * NP + (NP - 1), j, j == 1)
                    st = Steps(s_fin, b * FIN_STEPS + 1)
                    v.wait_ge(s_ssum, b + 1 + 1)
                    st.did(v.tensor_copy(sm[:, 4, :], W[3][:, :].rearrange("p (t c) -> p t c", c=P)[:, :, 0]))
                    rsqrt(v, st, sm[:, 5, :], sm[:, 4, :], sm[:, 6, :], sm[:, 7, :], float(NH * P), RMS_EPS)
                    st.wait(v)
                    assert st.n == FIN_STEPS
                    v.wait_ge(s_op, b * NH + NH + 1)
                    v.wait_ge(s_xres, b * 16 + 16)
                    v.wait_ge(s_x1out, b * 16 + 1)
                    for t in range(KT):
                        v.scalar_tensor_tensor(out=x1[:, t, :], in0=Y[t][:, :], scalar=sm[:, 5, t:t + 1],
                                               in1=x_res[:, t, :], op0=ALU.mult, op1=ALU.add).then_inc(s_x1, 1)


def tail(nc, c, ctx_rows, ctx_t, pad_mask, x1_dram, out):
    B, S, D = x1_dram.shape
    M = ctx_rows.shape[1]
    F = c.gate_sc.shape[1]
    KD, KT, KF = D // P, S // P, F // P
    T = B * KT
    FS = spans(F)
    out_tiles = out.rearrange("b (t p) d -> (b t) p d", p=P)
    NF = len(FS)
    assert NF % 2 == 1 and KT % 4 == 0 and KT == 4
    bank, ident = c.bank, c.ident
    ctx, sb, sem = scope(nc, "tail")
    with ctx:
        x1, x2 = sb("x1", [P, KT, D]), sb("x2", [P, KT, D])
        h, hT = sb("h", [P, D]), sb("hT", [P, KD, P])
        mem, memT = sb("mem", [P, B, D]), sb("memT", [P, B, KD, P])
        mk8 = sb("mk8", [P, B * M // 4], I32)
        mk, mneg, any_mk = sb("mk", [P, B * M]), sb("mneg", [P, B * M]), sb("any_mk", [P, B])
        stats, mv = sb("stats", [P, 2, 6]), sb("mv", [P, 2, 2])
        nr, rs, nb = sb("newton", [P, 4, 2]), sb("rstd", [P, 2]), sb("neg_mean_rstd", [P, 2])
        rx, sy = sb("rx", [P, 12]), sb("sy", [P, 2])
        kf = sb("kf", [P, 4, 2])
        sx, st_ = sb("sx", [P, 2]), sb("st", [P, 2])
        sc, pr, pT = sb("sc", [P, M]), sb("pr", [P, P]), sb("pT", [P, P])
        sxm = sb("softmax", [P, 8])
        xm, xv, xs = sb("xm", [P, D]), sb("xv", [P, D]), sb("xs", [P, D])
        xmag, xsum = sb("xmag", [P, D], U32), sb("xsum", [P, D])
        q16, qT = sb("q16", [P, D], BF16), sb("qT", [P, KD, P], BF16)
        g_, u_, sg, t_ = sb("g", [P, F]), sb("u", [P, F]), sb("sig", [P, F]), sb("t", [P, F])
        tv, ts_ = sb("tv", [P, F]), sb("ts", [P, F])
        tmag, tsum = sb("tmag", [P, F], U32), sb("tsum", [P, F])
        t16, tT = sb("t16", [P, F], BF16), sb("tT", [P, KF, P], BF16)
        yo = sb("yo", [P, 2, D])
        x3 = sb("x3", [P, 2, D])

        s_memT, s_mem, s_mask, s_pad, s_k = sem("memT_landed"), sem("mem_landed"), sem("mask_landed"), sem("pads_cleared"), sem("constants_ready")
        s_masks = sem("masks_ready")
        s_ld = [sem(f"x1_{t}_landed") for t in range(KT)]
        s_out = [sem(f"out{i}_stored") for i in range(2)]
        s_ln2, s_h, s_hs = sem("norm2_steps"), sem("h_ready"), sem("h_scale_ready")
        s_rstd, s_rs, s_sx, s_nb = sem("rstd_steps"), sem("rstd_ready"), sem("gate_up_scale_ready"), sem("bias_steps")
        s_hT, s_hTc, s_sc = sem("h_turned"), sem("h_turned_copied"), sem("scores_summed")
        s_soft, s_max, s_exp = sem("softmax_steps"), sem("max_ready"), sem("exp_ready")
        s_pT, s_pTc, s_rd = sem("p_turned"), sem("p_turned_copied"), sem("readout_summed")
        s_den, s_x2 = sem("denominator_steps"), sem("x2_ready")
        s_ln3, s_xr = sem("norm3_steps"), sem("x_scale_ready")
        s_xv, s_xs, s_xround, s_q = sem("x_scaled"), sem("x_scaled_small"), sem("x_rounding"), sem("x_quantised")
        s_qT, s_qTc, s_gu = sem("x_turned"), sem("x_turned_copied"), sem("gate_up_summed")
        s_g, s_u, s_sig = sem("g_ready"), sem("u_ready"), sem("g_sigmoid")
        s_gs, s_t = sem("silu_ready"), sem("t_ready")
        s_tr, s_tscale = sem("t_scale_steps"), sem("t_scale_ready")
        s_tv, s_ts, s_tround, s_tq = sem("t_scaled"), sem("t_scaled_small"), sem("t_rounding"), sem("t_quantised")
        s_tT, s_tTc, s_y = sem("t_turned"), sem("t_turned_copied"), sem("down_summed")
        s_yo, s_fin, s_ysc = sem("y_scaled"), sem("out_ready"), sem("y_scale_ready")
        s_xm, s_xrs = sem("x_centred"), sem("x_scale_steps")
        prime(nc, [s_x2, s_fin, s_hT, s_hTc, s_pT, s_pTc, s_qT, s_rd, s_q, s_gs, s_t, s_sig, s_tTc, s_tT, s_tv, s_ts,
                   s_xv, s_xs, s_yo, s_sc, s_exp, s_g, s_u, s_max, s_tq, *s_out, s_gu, s_y, s_ln2, s_soft, s_den,
                   s_ln3, s_tr, s_rstd, s_h, s_rs, s_sx, s_hs, s_nb, s_xround, s_tround, s_qTc, s_xr, s_tscale, s_xrs])

        RSTD = 6

        def batches(eng, step):
            for t in range(KT):
                step(t, t, 0, True, False)
            with eng.Fori(1, B - 1) as b:
                for t in range(KT):
                    step(b * KT + t, t, b, False, False)
            for t in range(KT):
                step((B - 1) * KT + t, t, B - 1, False, True)

        with nc.Block() as block:
            @block.sync
            def _(sp):
                def load(t, b):
                    sp.dma_start(x1[:, t, :], x1_dram[b, t * P:(t + 1) * P, :]).then_inc(s_ld[t], 16)

                def step(n, t, b, first, last):
                    if not last or t + 3 < KT:
                        sp.wait_ge(s_x2, n + 1)
                        load((t + 3) % KT, b + (t + 3) // KT)
                    if not first or t > 1:
                        store(n - 2, t)

                def store(n, t):
                    sp.wait_ge(s_fin, n + 2)
                    sp.dma_start(out_tiles[n], x3[:, t % 2, :]).then_inc(s_out[t % 2], 16)

                sp.dma_start(mk8[:, :], pad_mask.rearrange("b m -> () (b m)").to_broadcast([P, B * M // 4])
                             ).then_inc(s_mask, 16)
                for t in range(3):
                    load(t, 0)
                sp.wait_ge(s_pad, 3)
                for b in range(B):
                    sp.dma_start(memT[:, b, :, 0:M], ctx_t[b].rearrange("(k p) m -> p k m", p=P)).then_inc(s_memT, 16)
                sp.dma_start(mem[0:M, :, :], ctx_rows.rearrange("b m d -> m b d")).then_inc(s_mem, 16)
                batches(sp, step)
                store(T - 2, KT - 2)
                store(T - 1, KT - 1)
                for q in s_out:
                    sp.wait_ge(q, 16 * T // 2 + 1)

            @block.gpsimd
            def _(g):
                def silu_up(n):
                    for i, (a, w) in enumerate(FS):
                        g.wait_ge(s_sig, n * NF + i + 2)
                        g.tensor_tensor(g_[:, a:a + w], g_[:, a:a + w], sg[:, a:a + w], ALU.mult).then_inc(s_gs, 1)
                        g.wait_ge(s_gs, n * NF + i + 2)
                        g.wait_ge(s_u, n * NF + i + 2)
                        g.wait_ge(s_ts, n + 1)
                        g.tensor_tensor(t_[:, a:a + w], g_[:, a:a + w], u_[:, a:a + w], ALU.mult).then_inc(s_t, 1)

                def finish(n, t):
                    g.wait_ge(s_yo, n + 2)
                    g.wait_ge(s_out[t % 2], (n - t % 2) * 8 + 1)
                    g.tensor_tensor(x3[:, t % 2, :], yo[:, t % 2, :], x2[:, t, :], ALU.add).then_inc(s_fin, 1)

                def rstd(n3, n2):
                    calls = n2 if n2 is not None else n3 + 2
                    lo, hi = 0 if n2 is not None else 1, 2 if n3 is not None else 1
                    base = calls * RSTD + 1
                    x, xh, y, a = (nr[:, k, lo:hi] for k in range(4))
                    eps, half, three, minus = (kf[:, k, lo:hi] for k in range(4))
                    if n2 is not None:
                        g.wait_ge(s_ln2, n2 * 3 + 4)
                    if n3 is not None:
                        g.wait_ge(s_ln3, n3 * 3 + 4)
                    g.wait_ge(s_rs, calls + 1)

                    def did(n, ins):
                        ins.then_inc(s_rstd, 1)
                        g.wait_ge(s_rstd, base + n + 1)

                    did(0, g.tensor_tensor(x, mv[:, lo:hi, 1], eps, ALU.add))
                    did(1, g.tensor_tensor(xh, x, half, ALU.mult))
                    did(2, g.tensor_tensor(y, x, half, ALU.pow))
                    did(3, g.tensor_tensor(a, y, y, ALU.mult))
                    did(4, g.tensor_tensor(a, a, xh, ALU.mult))
                    did(5, g.tensor_tensor(a, a, three, ALU.add))
                    if n2 is not None:
                        g.wait_ge(s_h, n2 + 1)
                    if n3 is not None:
                        g.wait_ge(s_sx, n3 + 1)
                    g.tensor_tensor(rs[:, lo:hi], y, a, ALU.mult).then_inc(s_rs, 1)
                    if n2 is not None:
                        g.wait_ge(s_rs, calls + 2)
                        g.tensor_tensor(nb[:, 1:2], mv[:, 0, 0:1], rs[:, 0:1], ALU.mult).then_inc(s_nb, 1)
                        g.wait_ge(s_nb, n2 + 2)
                        g.tensor_tensor(nb[:, 0:1], nb[:, 1:2], minus[:, 0:1], ALU.mult).then_inc(s_hs, 1)

                def step(n, t, b, first, last):
                    if not last or t + 1 < KT:
                        rstd(n + 1, n + 3 if not last or t + 3 < KT else None)
                    silu_up(n)
                    if not first or t > 1:
                        finish(n - 2, (t + 2) % KT)

                g.memset(mem[:, :, :], 0.0).then_inc(s_pad, 1)
                g.memset(memT[:, :, :, :], 0.0).then_inc(s_pad, 1)
                g.memset(pr[:, :], 0.0).then_inc(s_pad, 1)
                for k, value in enumerate((LN_EPS, -0.5, 1.5, -1.0)):
                    g.memset(kf[:, k, :], value).then_inc(s_k, 1)
                g.wait_ge(s_k, 4)
                rstd(None, 0)
                rstd(None, 1)
                rstd(0, 2)
                batches(g, step)
                finish(T - 2, KT - 2)
                finish(T - 1, KT - 1)

            @block.scalar
            def _(act):
                def exp(n):
                    act.wait_ge(s_max, n + 2)
                    act.wait_ge(s_pT, n + 1)
                    nc.scalar.activation(pr[:, 0:M], sc[:, :], ACT.Exp, bias=sxm[:, 1:2],
                                         accum_out=sxm[:, 2:3]).then_inc(s_exp, 1)
                    act.wait_ge(s_pT, n + 2)
                    act.wait_ge(s_rd, n + 1)
                    nc.scalar.copy(pT[:, :], bank[5][:, 0:P]).then_inc(s_pTc, 1)

                def x_scaled(n):
                    act.wait_ge(s_xr, 2 * n + 3)
                    act.wait_ge(s_q, n + 1)
                    nc.scalar.activation(xv[:, :], xm[:, :], ACT.Copy, scale=rx[:, 6:7]).then_inc(s_xv, 1)
                    nc.scalar.activation(xs[:, :], xm[:, :], ACT.Copy, scale=rx[:, 7:8]).then_inc(s_xs, 1)

                def normed(n, t):
                    act.wait_ge(s_hs, n + 2)
                    act.wait_ge(s_hT, n + 1)
                    nc.scalar.activation(h[:, :], x1[:, t, :], ACT.Identity, bias=nb[:, 0:1],
                                         scale=rs[:, 0:1]).then_inc(s_h, 1)

                def h_turned(n):
                    act.wait_ge(s_hT, n + 2)
                    act.wait_ge(s_sc, n + 1)
                    nc.scalar.copy(hT[:, :, :], bank[4][:, :].rearrange("p (k i) -> p k i", i=P)).then_inc(s_hTc, 1)

                def x_turned(n):
                    act.wait_ge(s_qT, n + 2)
                    act.wait_ge(s_gu, n * 2 * NF + 1)
                    nc.scalar.copy(qT[:, :, :], bank[4][:, 0:KD * P // 2].bitcast(BF16)
                                   .rearrange("p (k i) -> p k i", i=P)).then_inc(s_qTc, 1)

                def t_turned(n):
                    act.wait_ge(s_y, n + 1)
                    for i in range(2):
                        k = min(8, KF - 8 * i)
                        act.wait_ge(s_tT, n * 2 + i + 2)
                        nc.scalar.copy(tT[:, 8 * i:8 * i + k, :], bank[4 + 2 * i][:, 0:k * P // 2].bitcast(BF16)
                                       .rearrange("p (k i) -> p k i", i=P)).then_inc(s_tTc, 1)

                def sigmoids(n):
                    for i, (a, w) in enumerate(FS):
                        act.wait_ge(s_g, n * NF + i + 2)
                        act.wait_ge(s_gs, n * NF + 1)
                        nc.scalar.activation(sg[:, a:a + w], g_[:, a:a + w], ACT.Sigmoid).then_inc(s_sig, 1)

                def t_scaled(n):
                    act.wait_ge(s_tscale, 2 * n + 3)
                    act.wait_ge(s_tq, n + 1)
                    nc.scalar.activation(tv[:, :], t_[:, :], ACT.Copy, scale=st_[:, 0:1]).then_inc(s_tv, 1)
                    nc.scalar.activation(ts_[:, :], t_[:, :], ACT.Copy, scale=st_[:, 1:2]).then_inc(s_ts, 1)

                def step(n, t, b, first, last):
                    if not last or t + 2 < KT:
                        exp(n + 2)
                    if not last or t + 3 < KT:
                        normed(n + 3, (t + 3) % KT)
                    sigmoids(n)
                    if not last or t + 1 < KT:
                        x_scaled(n + 1)
                    if not last or t + 3 < KT:
                        h_turned(n + 3)
                    if not last or t + 1 < KT:
                        x_turned(n + 1)
                    if not first or t > 0:
                        t_turned(n - 1)
                    t_scaled(n)

                act.wait_ge(s_pad, 3)
                normed(0, 0)
                h_turned(0)
                exp(0)
                normed(1, 1)
                h_turned(1)
                normed(2, 2)
                x_scaled(0)
                x_turned(0)
                exp(1)
                h_turned(2)
                batches(act, step)
                t_turned(T - 1)

            @block.tensor
            def _(pe):
                def scores(n, b):
                    pe.wait_ge(s_h, n + 2)
                    for k in range(KD):
                        mm = pe.transpose(bank[4][:, k * P:(k + 1) * P], h[:, k * P:(k + 1) * P], ident[:, :])
                    mm.then_inc(s_hT, 1)
                    pe.wait_ge(s_hTc, n + 2)
                    for k in range(KD):
                        mm = pe.matmul(bank[5][:, 0:P], hT[:, k, :], of_batch(memT, b, k), start=(k == 0),
                                       stop=(k == KD - 1))
                    mm.then_inc(s_sc, 1)

                def of_batch(m, b, k):
                    return m[:, b, k, :] if isinstance(b, int) else \
                        m[:, bass.ds(b, 1), k, :].rearrange("p o m -> p (o m)")

                def readout(n, b):
                    pe.wait_ge(s_exp, n + 2)
                    pe.transpose(bank[5][:, 0:P], pr[:, :], ident[:, :]).then_inc(s_pT, 1)
                    pe.wait_ge(s_pTc, n + 2)
                    pe.wait_ge(s_x2, n + 1)
                    rhs = mem[:, b, :] if isinstance(b, int) else \
                        mem[:, bass.ds(b, 1), :].rearrange("p o m -> p (o m)")
                    pe.matmul(bank[7][:, :], pT[:, :], rhs, start=True, stop=True).then_inc(s_rd, 1)

                def turn_x(n):
                    pe.wait_ge(s_q, n + 2)
                    for k in range(KD):
                        mm = pe.transpose(bank[4][:, k * 64:(k + 1) * 64].bitcast(BF16), q16[:, k * P:(k + 1) * P],
                                          c.ident_bf[:, :])
                    mm.then_inc(s_qT, 1)
                    pe.wait_ge(s_qTc, n + 2)

                def gate_up(n, t, chunks):
                    for i in chunks:
                        a, w = FS[i]
                        j = (t * NF + i) % 2
                        if not (isinstance(n, int) and n * NF + i < 2):
                            pe.wait_ge(s_u, n * NF + i)
                        for m, wT in enumerate((c.gateT, c.upT)):
                            for k in range(KD):
                                mm = pe.matmul(bank[2 * j + m][:, 0:w], qT[:, k, :], wT[:, k, a:a + w],
                                               start=(k == 0), stop=(k == KD - 1))
                            mm.then_inc(s_gu, 1)

                def down(n):
                    pe.wait_ge(s_tq, n + 2)
                    for k in range(KF):
                        if k == 8:
                            mm.then_inc(s_tT, 1)
                            pe.wait_ge(s_yo, n + 1)
                        mm = pe.transpose(bank[4 + 2 * (k // 8)][:, (k % 8) * 64:(k % 8 + 1) * 64].bitcast(BF16),
                                          t16[:, k * P:(k + 1) * P], c.ident_bf[:, :])
                    mm.then_inc(s_tT, 1)
                    pe.wait_ge(s_tTc, n * 2 + 3)
                    for k in range(KF):
                        mm = pe.matmul(bank[6][:, :], tT[:, k, :], c.downT[:, k, :], start=(k == 0), stop=(k == KF - 1))
                    mm.then_inc(s_y, 1)

                def step(n, t, b, first, last):
                    gate_up(n, t, range(2, NF))
                    if not last or t + 2 < KT:
                        readout(n + 2, b + (t + 2) // KT)
                    if not last or t + 3 < KT:
                        scores(n + 3, b + (t + 3) // KT)
                    if not last or t + 1 < KT:
                        turn_x(n + 1)
                        gate_up(n + 1, (t + 1) % KT, range(2))
                    if not first or t > 0:
                        down(n - 1)

                pe.wait_ge(s_pad, 3)
                pe.wait_ge(s_memT, 16 * B)
                pe.wait_ge(s_mem, 16)
                scores(0, 0)
                readout(0, 0)
                scores(1, 0)
                turn_x(0)
                gate_up(0, 0, range(2))
                readout(1, 0)
                scores(2, 0)
                batches(pe, step)
                down(T - 1)

            @block.vector
            def _(v):
                def wait_did(s, ins, base, n):
                    ins.then_inc(s, 1)
                    v.wait_ge(s, base + n + 1)

                def norms(n3, n2, t, b):
                    parts = [(0, n2, s_ln2, x1, t)] * (n2 is not None) + [(1, n3, s_ln3, x2, (t - 2) % KT)] * (n3 is not None)
                    if n2 is not None:
                        v.wait_ge(s_ld[t], b * 16 + 16)
                    v.wait_ge(s_rs, (n2 if n2 is not None else n3 + 2) + 1)
                    if n2 is not None:
                        v.wait_ge(s_hs, n2 + 1)
                    for i, n, s, x, slot in parts:
                        v.bn_stats(stats[:, i, :], x[:, slot, :]).then_inc(s, 1)
                    for i, n, s, x, slot in parts:
                        v.wait_ge(s, n * 3 + 2)
                        v.tensor_copy(rx[:, 8 + i:9 + i], stats[:, i, 0:1]).then_inc(s, 1)
                    for i, n, s, x, slot in parts:
                        v.bn_aggr(mv[:, i, :], stats[:, i, :]).then_inc(s, 1)
                    if n3 is not None:
                        v.wait_ge(s_ln3, n3 * 3 + 4)
                        v.wait_ge(s_xs, n3 + 1)
                        v.scalar_tensor_tensor(out=xm[:, :], in0=x2[:, (t - 2) % KT, :], scalar=mv[:, 1, 0:1],
                                               in1=c.up_named[:, :], op0=ALU.subtract, op1=ALU.mult).then_inc(s_xm, 1)

                def x_scale(n):
                    v.wait_ge(s_xm, n + 1)
                    xr = n * 2 + 1
                    wait_did(s_xrs, v.tensor_reduce(rx[:, 4:5], xm[:, :], AX, ALU.max, apply_absolute_value=True), xr, 0)
                    wait_did(s_xrs, v.reciprocal(rx[:, 5:6], rx[:, 4:5]), xr, 1)
                    v.tensor_scalar(rx[:, 6:7], rx[:, 5:6], FP8_MAX, None, ALU.mult).then_inc(s_xr, 1)
                    v.tensor_scalar(rx[:, 7:8], rx[:, 5:6], FP8_MAX * SMALL, None, ALU.mult).then_inc(s_xr, 1)

                def gate_up_scale(n):
                    v.wait_ge(s_rs, n + 2 + 2)
                    v.tensor_scalar(sx[:, 0:1], rx[:, 4:5], rs[:, 1:2], -4.0 / (SMALL * FP8_MAX),
                                    ALU.mult, ALU.mult).then_inc(s_sx, 1)

                def softmax(n, b):
                    base = n * 3 + 1
                    col = bass.ts(b, M)
                    v.wait_ge(s_sc, n + 2)
                    v.wait_ge(s_exp, n + 1)
                    wait_did(s_soft, v.scalar_tensor_tensor(out=sc[:, :], in0=bank[5][:, 0:M], scalar=float(D) ** -0.5,
                                                            in1=mk[:, col], op0=ALU.mult, op1=ALU.mult), base, 0)
                    wait_did(s_soft, v.tensor_tensor(sc[:, :], sc[:, :], mneg[:, col], ALU.add), base, 1)
                    wait_did(s_soft, v.tensor_reduce(sxm[:, 0:1], sc[:, :], AX, ALU.max), base, 2)
                    v.tensor_scalar(sxm[:, 1:2], sxm[:, 0:1], -1.0, None, ALU.mult).then_inc(s_max, 1)

                def denominator(n, b):
                    base = n * 2 + 1
                    v.wait_ge(s_exp, n + 2)
                    wait_did(s_den, v.reciprocal(sxm[:, 3:4], sxm[:, 2:3]), base, 0)
                    wait_did(s_den, v.tensor_tensor(sxm[:, 4:5], sxm[:, 3:4], any_mk[:, bass.ds(b, 1)], ALU.mult),
                             base, 1)

                def add_readout(n, t):
                    v.wait_ge(s_rd, n + 2)
                    v.wait_ge(s_fin, n - 4 + 2) if not (isinstance(n, int) and n < 4) else None
                    v.scalar_tensor_tensor(out=x2[:, t, :], in0=bank[7][:, :], scalar=sxm[:, 4:5], in1=x1[:, t, :],
                                           op0=ALU.mult, op1=ALU.add).then_inc(s_x2, 1)
                    v.wait_ge(s_x2, n + 2)

                def x_round(n):
                    v.wait_ge(s_xv, n + 2)
                    v.wait_ge(s_xs, n + 2)
                    v.wait_ge(s_qT, n + 1)
                    v.wait_ge(s_q, n + 1)
                    round_e4m3(v, s_xround, n * 2 + 1, xv[:, :], xs[:, :], xmag[:, :], xsum[:, :], q16[:, :], s_q)

                def scaled_gate_up(n, t):
                    for i, (a, w) in enumerate(FS):
                        j = (t * NF + i) % 2
                        v.wait_ge(s_gu, n * 2 * NF + 2 * i + 3)
                        v.wait_ge(s_t, n * NF + 1)
                        v.wait_ge(s_sx, n + 2)
                        v.scalar_tensor_tensor(out=g_[:, a:a + w], in0=bank[2 * j][:, 0:w], scalar=sx[:, 0:1],
                                               in1=c.gate_sc[:, a:a + w], op0=ALU.mult, op1=ALU.mult).then_inc(s_g, 1)
                        v.scalar_tensor_tensor(out=u_[:, a:a + w], in0=bank[2 * j + 1][:, 0:w], scalar=sx[:, 0:1],
                                               in1=c.up_sc[:, a:a + w], op0=ALU.mult, op1=ALU.mult).then_inc(s_u, 1)

                def t_scale(n, t):
                    base = n * 2 + 1
                    v.wait_ge(s_t, n * NF + NF + 1)
                    v.wait_ge(s_ts, n + 1)
                    wait_did(s_tr, v.tensor_reduce(rx[:, 9:10], t_[:, :], AX, ALU.max, apply_absolute_value=True),
                             base, 0)
                    wait_did(s_tr, v.reciprocal(rx[:, 10:11], rx[:, 9:10]), base, 1)
                    v.tensor_scalar(st_[:, 0:1], rx[:, 10:11], FP8_MAX, None, ALU.mult).then_inc(s_tscale, 1)
                    v.tensor_scalar(st_[:, 1:2], rx[:, 10:11], FP8_MAX * SMALL, None, ALU.mult).then_inc(s_tscale, 1)
                    v.tensor_scalar(sy[:, t % 2:t % 2 + 1], rx[:, 9:10], -4.0 / (SMALL * FP8_MAX), None,
                                    ALU.mult).then_inc(s_ysc, 1)

                def t_round(n):
                    v.wait_ge(s_tv, n + 2)
                    v.wait_ge(s_ts, n + 2)
                    v.wait_ge(s_tT, n * 2 + 1)
                    v.wait_ge(s_tq, n + 1)
                    round_e4m3(v, s_tround, n * 2 + 1, tv[:, :], ts_[:, :], tmag[:, :], tsum[:, :], t16[:, :], s_tq)

                def y_scaled(n, t):
                    v.wait_ge(s_y, n + 2)
                    v.wait_ge(s_ysc, n + 1)
                    if not (isinstance(n, int) and n < 2):
                        v.wait_ge(s_fin, n)
                    v.scalar_tensor_tensor(out=yo[:, t % 2, :], in0=bank[6][:, :], scalar=sy[:, t % 2:t % 2 + 1],
                                           in1=c.down_sc[:, :], op0=ALU.mult, op1=ALU.mult).then_inc(s_yo, 1)

                def step(n, t, b, first, last):
                    if not last or t + 1 < KT:
                        add_readout(n + 1, (t + 1) % KT)
                    if not last or t + 2 < KT:
                        softmax(n + 2, b + (t + 2) // KT)
                    if not last or t + 1 < KT:
                        norms(n + 1, n + 3 if not last or t + 3 < KT else None, (t + 3) % KT, b + (t + 3) // KT)
                    scaled_gate_up(n, t)
                    if not last or t + 1 < KT:
                        x_scale(n + 1)
                    if not last or t + 2 < KT:
                        denominator(n + 2, b + (t + 2) // KT)
                    if not first or t > 1:
                        y_scaled(n - 2, (t + 2) % KT)
                    if not last or t + 1 < KT:
                        x_round(n + 1)
                        gate_up_scale(n + 1)
                    if not first or t > 0:
                        t_round(n - 1)
                    t_scale(n, t)

                v.wait_ge(s_mask, 16)
                v.tensor_copy(mk[:, :], mk8[:, :].bitcast(U8)).then_inc(s_masks, 1)
                v.wait_ge(s_masks, 1)
                v.tensor_scalar(mneg[:, :], mk[:, :], -1.0, NEG, ALU.add, ALU.mult).then_inc(s_masks, 1)
                v.tensor_reduce(any_mk[:, :], mk[:, :].rearrange("p (b m) -> p b m", m=M), AX, ALU.max
                                ).then_inc(s_masks, 1)
                v.wait_ge(s_masks, 3)
                norms(None, 0, 0, 0)
                softmax(0, 0)
                norms(None, 1, 1, 0)
                denominator(0, 0)
                add_readout(0, 0)
                norms(0, 2, 2, 0)
                x_scale(0)
                x_round(0)
                gate_up_scale(0)
                softmax(1, 0)
                denominator(1, 0)
                batches(v, step)
                y_scaled(T - 2, KT - 2)
                t_round(T - 1)
                y_scaled(T - 1, KT - 1)


def kernel(x, ctx_2048, mask_BxS2_bk0, L0_attn_slope_rate, L0_attn_w_qkv, L0_attn_w_gate, L0_attn_w_out,
           L0_attn_norm_w, L0_ffn_w_gate, L0_ffn_w_up, L0_ffn_w_down, L0_ffn_up_reorder_index,
           L0_ffn_down_reorder_index):
    import concourse.bacc as bacc
    from concourse.bass_utils import run_bass_kernel_spmd

    x, ctx = np.asarray(x), np.asarray(ctx_2048)
    D = x.shape[2]
    NH = np.asarray(L0_attn_slope_rate).shape[0]
    KD, NP = D // P, NH // 2
    wq = np.asarray(L0_attn_w_qkv).reshape(NP, 2, 3, P, KD, P)
    wq = wq.transpose(0, 5, 4, 1, 2, 3)
    part0 = np.stack([wq[:, :, :, 0, 0], wq[:, :, :, 0, 1], wq[:, :, :, 0, 2], wq[:, :, :, 1, 2]], axis=3)
    part1 = np.stack([wq[:, :, :, 1, 0], wq[:, :, :, 1, 1]], axis=3)
    gates = np.asarray(L0_attn_w_gate).reshape(NP, 2 * P, KD, P).transpose(0, 3, 2, 1)
    outs = np.asarray(L0_attn_w_out).reshape(D, NP, 2, P).transpose(1, 3, 2, 0)
    arrays = {
        "x": x,
        "ctx": ctx,
        "ctx_t": ctx.transpose(0, 2, 1),
        "pad_mask": np.ascontiguousarray(mask_BxS2_bk0).view(np.int32),
        "slope": np.asarray(L0_attn_slope_rate).reshape(1, NH),
        "w_part0": part0.reshape(NP, P, -1),
        "w_part1": part1.reshape(NP, P, -1),
        "w_gates": gates.reshape(NP, P, -1),
        "w_outs": outs.reshape(NP, P, -1),
        "norm_w": np.asarray(L0_attn_norm_w).reshape(NH, P).T,
        "f_gate": np.asarray(L0_ffn_w_gate),
        "f_up": np.asarray(L0_ffn_w_up),
        "f_down": np.asarray(L0_ffn_w_down),
        "up_idx": np.asarray(L0_ffn_up_reorder_index).reshape(-1, P).T,
        "down_idx": np.asarray(L0_ffn_down_reorder_index).reshape(-1, P).T,
    }
    arrays = {f"in_{k}": np.ascontiguousarray(a) for k, a in arrays.items()}
    nc = bacc.Bacc("TRN2", target_bir_lowering=False, num_devices=1)
    args = [nc.dram_tensor(k, a.shape, mybir.dt.from_np(a.dtype), kind="ExternalInput").ap()
            for k, a in arrays.items()]
    out = nc.dram_tensor("out", x.shape, F32, kind="ExternalOutput").ap()
    layer(nc, *args, out)
    r = run_bass_kernel_spmd(nc, [arrays], core_ids=[0])
    return r.results[0]["out"]
```
